# Optimizing a Trainium2 kernel written in Bass

```python
import numpy as np
import jax
import jax.numpy as jnp

def _softmax(x, axis=-1):
    return jax.nn.softmax(x, axis=axis)

def _gelu(x):
    return jax.nn.gelu(x, approximate=True)

def _silu(x):
    return jax.nn.silu(x)

def _sigmoid(x):
    return jax.nn.sigmoid(x)

def _layernorm(x, axis=-1, eps=1e-05):
    m = jnp.mean(x, axis=axis, keepdims=True)
    v = jnp.var(x, axis=axis, keepdims=True)
    return (x - m) / jnp.sqrt(v + eps)

def _scatter_add(tgt, idx, src, axis=0):
    return tgt.at[idx].add(src)

def _segment_sum(src, seg, n):
    return jax.ops.segment_sum(src, seg, n)
kernel_name = 'mk_adj_ffn_d4_adj_r2_c698bf'

def setup_inputs(seed: int=0):
    np.random.seed(seed)
    _w = jnp.asarray

    def _rec_inputs():
        import jax
        import jax.numpy as jnp
        _gk = jax.random.key(seed)
        x = -0.0005207 + 1.001 * jax.random.normal(jax.random.fold_in(_gk, 1), (1354, 128), jnp.float32)
        _a = jax.random.bernoulli(jax.random.fold_in(_gk, 2), 0.0118168, (1354, 1354))
        _a = jnp.logical_or(_a, jnp.swapaxes(_a, -1, -2))
        _a = jnp.logical_or(_a, jnp.eye(1354, dtype=bool))
        adj = _a.astype(jnp.int32)
        return (x, adj)
    x, adj = _rec_inputs()

    def _L0_gnn_setup():
        import jax, jax.numpy as jnp
        import numpy as np
        N = 4096
        IN_F = 128
        OUT_F = 128
        ALPHA = 0.2
        NEG_INF = -1000000000000.0

        def _xavier(key, shape, gain=1.414):
            fan_in, fan_out = (shape[0], shape[1])
            bound = gain * np.sqrt(6.0 / (fan_in + fan_out))
            return jax.random.uniform(key, shape, jnp.float32, -bound, bound)
        key = jax.random.key(seed)
        k1, k2, k3, k4 = jax.random.split(key, 4)
        inp = jax.random.normal(k1, (N, IN_F), jnp.float32)
        adj = jax.random.randint(k2, (N, N), 0, 2, jnp.int32)
        W = _xavier(k3, (IN_F, OUT_F))
        a = _xavier(k4, (2 * OUT_F, 1))
        return {'inp': inp, 'adj': adj, 'W': W, 'a': a}
    _L0_gnn_all = _L0_gnn_setup()
    _L0_gnn_in = {k: v for k, v in _L0_gnn_all.items() if k in ('W', 'a')}
    del _L0_gnn_all

    def _L0_ffn_setup():
        import jax, jax.numpy as jnp
        import numpy as np
        D_MODEL = 128
        EXPERT_DIM = 256
        NUM_EXPERTS = 8
        TOP_K = 2
        SEQ_LEN = 1024
        BATCH = 2
        key = jax.random.key(seed)
        ks = jax.random.split(key, 8)
        s = 0.02
        x = jax.random.normal(ks[0], (SEQ_LEN, BATCH, D_MODEL), dtype=jnp.float32)
        Wg = jax.random.normal(ks[1], (D_MODEL, NUM_EXPERTS), dtype=jnp.float32) * s
        bg = jax.random.normal(ks[2], (NUM_EXPERTS,), dtype=jnp.float32) * s
        bias = jnp.zeros((NUM_EXPERTS,), dtype=jnp.float32)
        W1 = jax.random.normal(ks[3], (NUM_EXPERTS, D_MODEL, EXPERT_DIM), dtype=jnp.float32) * s
        b1 = jax.random.normal(ks[4], (NUM_EXPERTS, EXPERT_DIM), dtype=jnp.float32) * s
        W2 = jax.random.normal(ks[5], (NUM_EXPERTS, EXPERT_DIM, D_MODEL), dtype=jnp.float32) * s
        b2 = jax.random.normal(ks[6], (NUM_EXPERTS, D_MODEL), dtype=jnp.float32) * s
        return {'x': x, 'Wg': Wg, 'bg': bg, 'bias': bias, 'W1': W1, 'b1': b1, 'W2': W2, 'b2': b2}
    _L0_ffn_all = _L0_ffn_setup()
    _L0_ffn_in = {k: v for k, v in _L0_ffn_all.items() if k in ('Wg', 'bg', 'bias', 'W1', 'b1', 'W2', 'b2')}
    del _L0_ffn_all

    def _L1_gnn_setup():
        import jax, jax.numpy as jnp
        import numpy as np
        N = 2048
        INP_DIM = 128
        EMB_DIM = 128
        ALPHA = 0.01
        NEG_INF = -9000000000000000.0

        def _xavier(key, shape, gain=1.414):
            fan_in, fan_out = (shape[0], shape[1])
            limit = gain * np.sqrt(6.0 / (fan_in + fan_out))
            return jax.random.uniform(key, shape, jnp.float32, -limit, limit)

        def _gat_layer(h, adj, W, a):
            Wh = h @ W
            F_out = Wh.shape[1]
            f1 = Wh @ a[:F_out]
            f2 = Wh @ a[F_out:]
            e = jax.nn.leaky_relu(f1 + f2.T, ALPHA)
            att = jnp.where(adj > 0, e, NEG_INF)
            att = jax.nn.softmax(att, axis=1)
            h_prime = att @ Wh
            return jax.nn.elu(h_prime)
        key = jax.random.key(seed)
        ks = jax.random.split(key, 9)
        inp = {'input': jax.random.normal(ks[0], (N, INP_DIM), jnp.float32), 'adj': jax.random.randint(ks[1], (N, N), 0, 2, jnp.int32), 'W0': _xavier(ks[2], (INP_DIM, EMB_DIM)), 'W1': _xavier(ks[3], (EMB_DIM, EMB_DIM)), 'a1': _xavier(ks[4], (2 * EMB_DIM, 1)), 'W2': _xavier(ks[5], (EMB_DIM, EMB_DIM)), 'a2': _xavier(ks[6], (2 * EMB_DIM, 1)), 'W3': _xavier(ks[7], (EMB_DIM, EMB_DIM)), 'a3': _xavier(ks[8], (2 * EMB_DIM, 1))}
        return inp
    _L1_gnn_all = _L1_gnn_setup()
    _L1_gnn_in = {k: v for k, v in _L1_gnn_all.items() if k in ('W0', 'W1', 'a1', 'W2', 'a2', 'W3', 'a3')}
    del _L1_gnn_all

    def _L1_ffn_setup():
        import jax, jax.numpy as jnp
        import numpy as np
        E, D, H, TOP_K = (6, 128, 128, 2)
        ROUTER_H = D // 2
        key = jax.random.key(seed)
        ks = jax.random.split(key, 12)
        s = 1.0 / np.sqrt(D)
        sh = 1.0 / np.sqrt(H)
        sr = 1.0 / np.sqrt(ROUTER_H)
        return {'features': jax.random.normal(ks[0], (8, 2048, D), dtype=jnp.float32), 'router_w1': jax.random.uniform(ks[1], (D, ROUTER_H), jnp.float32, -s, s), 'router_b1': jnp.zeros((ROUTER_H,), jnp.float32), 'router_w2': jax.random.uniform(ks[2], (ROUTER_H, E), jnp.float32, -sr, sr), 'router_b2': jnp.zeros((E,), jnp.float32), 'expert_w1': jax.random.uniform(ks[3], (E, D, H), jnp.float32, -s, s), 'expert_b1': jnp.zeros((E, H), jnp.float32), 'expert_w2': jax.random.uniform(ks[4], (E, H, H), jnp.float32, -sh, sh), 'expert_b2': jnp.zeros((E, H), jnp.float32), 'expert_w3': jax.random.uniform(ks[5], (E, H, D), jnp.float32, -sh, sh), 'expert_b3': jnp.zeros((E, D), jnp.float32)}
    _L1_ffn_all = _L1_ffn_setup()
    _L1_ffn_in = {k: v for k, v in _L1_ffn_all.items() if k in ('router_w1', 'router_b1', 'router_w2', 'router_b2', 'expert_w1', 'expert_b1', 'expert_w2', 'expert_b2', 'expert_w3', 'expert_b3')}
    del _L1_ffn_all

    def _L2_gnn_setup():
        import jax, jax.numpy as jnp
        import numpy as np
        N = 2048
        IN_F = 128
        OUT_F = 128
        HEADS = 4
        HEAD_DIM = OUT_F // HEADS
        ALPHA = 0.2
        NEG_INF = -9000000000000000.0
        LN_EPS = 1e-05
        key = jax.random.key(seed)
        k1, k2, k3, k4 = jax.random.split(key, 4)
        x = jax.random.normal(k1, (N, IN_F), dtype=jnp.float32)
        adj = jax.random.randint(k2, (N, N), 0, 2, dtype=jnp.int32)

        def xavier(k, shape, gain=1.414):
            fan_in, fan_out = (shape[0], shape[1])
            bound = gain * np.sqrt(6.0 / (fan_in + fan_out))
            return jax.random.uniform(k, shape, jnp.float32, -bound, bound)
        W = xavier(k3, (IN_F, OUT_F))
        a = xavier(k4, (2 * HEAD_DIM, 1))
        gamma = jnp.ones((OUT_F,), jnp.float32)
        beta = jnp.zeros((OUT_F,), jnp.float32)
        return {'x': x, 'adj': adj, 'W': W, 'a': a, 'gamma': gamma, 'beta': beta}
    _L2_gnn_all = _L2_gnn_setup()
    _L2_gnn_in = {k: v for k, v in _L2_gnn_all.items() if k in ('W', 'a', 'gamma', 'beta')}
    del _L2_gnn_all

    def _L2_ffn_setup():
        import jax, jax.numpy as jnp
        import numpy as np
        IN_CH = 128
        OUT_CH = 128
        key = jax.random.key(seed)
        kx, kw, kb = jax.random.split(key, 3)
        x = jax.random.normal(kx, (8, 2048, IN_CH), dtype=jnp.float32)
        bound = 1.0 / np.sqrt(IN_CH)
        weight = jax.random.uniform(kw, (OUT_CH, IN_CH), dtype=jnp.float32, minval=-bound, maxval=bound)
        bias = jax.random.uniform(kb, (OUT_CH,), dtype=jnp.float32, minval=-bound, maxval=bound)
        return {'x': x, 'weight': weight, 'bias': bias}
    _L2_ffn_all = _L2_ffn_setup()
    _L2_ffn_in = {k: v for k, v in _L2_ffn_all.items() if k in ('weight', 'bias')}
    del _L2_ffn_all

    def _L3_gnn_setup():
        import jax, jax.numpy as jnp
        import numpy as np
        ALPHA = 0.2
        NEG_INF = -9000000000000000.0
        N, F_IN, F_OUT = (4096, 128, 128)
        key = jax.random.key(seed)
        k_h, k_adj, k_W, k_a = jax.random.split(key, 4)
        h = jax.random.normal(k_h, (N, F_IN), dtype=jnp.float32)
        adj = jax.random.randint(k_adj, (N, N), 0, 2, dtype=jnp.int32)
        gain = 1.414
        limit_W = gain * np.sqrt(6.0 / (F_IN + F_OUT))
        W = jax.random.uniform(k_W, (F_IN, F_OUT), dtype=jnp.float32, minval=-limit_W, maxval=limit_W)
        limit_a = gain * np.sqrt(6.0 / (2 * F_OUT + 1))
        a = jax.random.uniform(k_a, (2 * F_OUT, 1), dtype=jnp.float32, minval=-limit_a, maxval=limit_a)
        return {'h': h, 'adj': adj, 'W': W, 'a': a}
    _L3_gnn_all = _L3_gnn_setup()
    _L3_gnn_in = {k: v for k, v in _L3_gnn_all.items() if k in ('W', 'a')}
    del _L3_gnn_all

    def _L3_ffn_setup():
        import jax, jax.numpy as jnp
        import numpy as np
        D_MODEL = 128
        N_EXPERTS = 16
        HIDDEN = 256
        SCALE = 0.02
        key = jax.random.key(seed)
        ks = jax.random.split(key, 5)
        x = jax.random.normal(ks[0], (4, 4096, D_MODEL), dtype=jnp.float32)
        gate_w = jax.random.normal(ks[1], (D_MODEL, N_EXPERTS), dtype=jnp.float32) * SCALE
        gate_b = jnp.zeros((N_EXPERTS,), dtype=jnp.float32)
        w1 = jax.random.normal(ks[2], (N_EXPERTS, D_MODEL, HIDDEN), dtype=jnp.float32) * SCALE
        w2 = jax.random.normal(ks[3], (N_EXPERTS, D_MODEL, HIDDEN), dtype=jnp.float32) * SCALE
        w3 = jax.random.normal(ks[4], (N_EXPERTS, HIDDEN, D_MODEL), dtype=jnp.float32) * SCALE
        return {'x': x, 'gate_w': gate_w, 'gate_b': gate_b, 'w1': w1, 'w2': w2, 'w3': w3}
    _L3_ffn_all = _L3_ffn_setup()
    _L3_ffn_in = {k: v for k, v in _L3_ffn_all.items() if k in ('gate_w', 'gate_b', 'w1', 'w2', 'w3')}
    del _L3_ffn_all
    return {'x': x, 'adj': adj, 'L0_gnn_W': _L0_gnn_in['W'], 'L0_gnn_a': _L0_gnn_in['a'], 'L0_ffn_Wg': _L0_ffn_in['Wg'], 'L0_ffn_bg': _L0_ffn_in['bg'], 'L0_ffn_bias': _L0_ffn_in['bias'], 'L0_ffn_W1': _L0_ffn_in['W1'], 'L0_ffn_b1': _L0_ffn_in['b1'], 'L0_ffn_W2': _L0_ffn_in['W2'], 'L0_ffn_b2': _L0_ffn_in['b2'], 'L1_gnn_W0': _L1_gnn_in['W0'], 'L1_gnn_W1': _L1_gnn_in['W1'], 'L1_gnn_a1': _L1_gnn_in['a1'], 'L1_gnn_W2': _L1_gnn_in['W2'], 'L1_gnn_a2': _L1_gnn_in['a2'], 'L1_gnn_W3': _L1_gnn_in['W3'], 'L1_gnn_a3': _L1_gnn_in['a3'], 'L1_ffn_router_w1': _L1_ffn_in['router_w1'], 'L1_ffn_router_b1': _L1_ffn_in['router_b1'], 'L1_ffn_router_w2': _L1_ffn_in['router_w2'], 'L1_ffn_router_b2': _L1_ffn_in['router_b2'], 'L1_ffn_expert_w1': _L1_ffn_in['expert_w1'], 'L1_ffn_expert_b1': _L1_ffn_in['expert_b1'], 'L1_ffn_expert_w2': _L1_ffn_in['expert_w2'], 'L1_ffn_expert_b2': _L1_ffn_in['expert_b2'], 'L1_ffn_expert_w3': _L1_ffn_in['expert_w3'], 'L1_ffn_expert_b3': _L1_ffn_in['expert_b3'], 'L2_gnn_W': _L2_gnn_in['W'], 'L2_gnn_a': _L2_gnn_in['a'], 'L2_gnn_gamma': _L2_gnn_in['gamma'], 'L2_gnn_beta': _L2_gnn_in['beta'], 'L2_ffn_weight': _L2_ffn_in['weight'], 'L2_ffn_bias': _L2_ffn_in['bias'], 'L3_gnn_W': _L3_gnn_in['W'], 'L3_gnn_a': _L3_gnn_in['a'], 'L3_ffn_gate_w': _L3_ffn_in['gate_w'], 'L3_ffn_gate_b': _L3_ffn_in['gate_b'], 'L3_ffn_w1': _L3_ffn_in['w1'], 'L3_ffn_w2': _L3_ffn_in['w2'], 'L3_ffn_w3': _L3_ffn_in['w3']}

def reference(x, adj, L0_gnn_W, L0_gnn_a, L0_ffn_Wg, L0_ffn_bg, L0_ffn_bias, L0_ffn_W1, L0_ffn_b1, L0_ffn_W2, L0_ffn_b2, L1_gnn_W0, L1_gnn_W1, L1_gnn_a1, L1_gnn_W2, L1_gnn_a2, L1_gnn_W3, L1_gnn_a3, L1_ffn_router_w1, L1_ffn_router_b1, L1_ffn_router_w2, L1_ffn_router_b2, L1_ffn_expert_w1, L1_ffn_expert_b1, L1_ffn_expert_w2, L1_ffn_expert_b2, L1_ffn_expert_w3, L1_ffn_expert_b3, L2_gnn_W, L2_gnn_a, L2_gnn_gamma, L2_gnn_beta, L2_ffn_weight, L2_ffn_bias, L3_gnn_W, L3_gnn_a, L3_ffn_gate_w, L3_ffn_gate_b, L3_ffn_w1, L3_ffn_w2, L3_ffn_w3):
    import jax
    import jax.numpy as jnp

    def _L0_gnn_ref(inp, adj, W, a):
        import jax, jax.numpy as jnp
        import numpy as np
        N = 4096
        IN_F = 128
        OUT_F = 128
        ALPHA = 0.2
        NEG_INF = -1000000000000.0

        def _xavier(key, shape, gain=1.414):
            fan_in, fan_out = (shape[0], shape[1])
            bound = gain * np.sqrt(6.0 / (fan_in + fan_out))
            return jax.random.uniform(key, shape, jnp.float32, -bound, bound)
        h = inp @ W
        a1 = a[:OUT_F, 0]
        a2 = a[OUT_F:, 0]
        s1 = h @ a1
        s2 = h @ a2
        e = jax.nn.leaky_relu(s1[:, None] + s2[None, :], negative_slope=ALPHA)
        att = jnp.where(adj > 0, e, NEG_INF)
        att = jax.nn.softmax(att, axis=1)
        h_prime = att @ h
        return jax.nn.elu(h_prime)

    def _L0_ffn_ref(x, Wg, bg, bias, W1, b1, W2, b2):
        import jax, jax.numpy as jnp
        import numpy as np
        D_MODEL = 128
        EXPERT_DIM = 256
        NUM_EXPERTS = 8
        TOP_K = 2
        SEQ_LEN = 1024
        BATCH = 2
        x_flat = x.reshape(-1, D_MODEL)
        gate_logits = x_flat @ Wg + bg + bias
        topk_vals, topk_idx = jax.lax.top_k(gate_logits, TOP_K)
        topk_w = jax.nn.softmax(topk_vals, axis=-1)
        combine = (jax.nn.one_hot(topk_idx, NUM_EXPERTS, dtype=x.dtype) * topk_w[..., None]).sum(axis=1)
        h = jax.nn.relu(jnp.einsum('td,edh->teh', x_flat, W1) + b1)
        y = jnp.einsum('teh,ehd->ted', h, W2) + b2
        out = jnp.einsum('ted,te->td', y, combine)
        return out.reshape(x.shape)

    def _L1_gnn_ref(input, adj, W0, W1, a1, W2, a2, W3, a3):
        import jax, jax.numpy as jnp
        import numpy as np
        N = 2048
        INP_DIM = 128
        EMB_DIM = 128
        ALPHA = 0.01
        NEG_INF = -9000000000000000.0

        def _xavier(key, shape, gain=1.414):
            fan_in, fan_out = (shape[0], shape[1])
            limit = gain * np.sqrt(6.0 / (fan_in + fan_out))
            return jax.random.uniform(key, shape, jnp.float32, -limit, limit)

        def _gat_layer(h, adj, W, a):
            Wh = h @ W
            F_out = Wh.shape[1]
            f1 = Wh @ a[:F_out]
            f2 = Wh @ a[F_out:]
            e = jax.nn.leaky_relu(f1 + f2.T, ALPHA)
            att = jnp.where(adj > 0, e, NEG_INF)
            att = jax.nn.softmax(att, axis=1)
            h_prime = att @ Wh
            return jax.nn.elu(h_prime)
        h = input @ W0
        h = _gat_layer(h, adj, W1, a1)
        h = _gat_layer(h, adj, W2, a2)
        h = _gat_layer(h, adj, W3, a3)
        return h

    def _L1_ffn_ref(features, router_w1, router_b1, router_w2, router_b2, expert_w1, expert_b1, expert_w2, expert_b2, expert_w3, expert_b3):
        import jax, jax.numpy as jnp
        import numpy as np
        E, D, H, TOP_K = (6, 128, 128, 2)
        ROUTER_H = D // 2
        rh = jax.nn.relu(features @ router_w1 + router_b1)
        expert_logits = jax.nn.softmax(rh @ router_w2 + router_b2, axis=-1)
        top_w, top_i = jax.lax.top_k(expert_logits, TOP_K)
        routing_weights = jax.nn.softmax(top_w, axis=-1)
        h1 = jax.nn.relu(jnp.einsum('bsd,edh->bseh', features, expert_w1) + expert_b1)
        h2 = jax.nn.relu(jnp.einsum('bseh,ehf->bsef', h1, expert_w2) + expert_b2)
        expert_out = jnp.einsum('bsef,efo->bseo', h2, expert_w3) + expert_b3
        sel = jnp.take_along_axis(expert_out, top_i[:, :, :, None], axis=2)
        combined = jnp.sum(sel * routing_weights[..., None], axis=2)
        return combined

    def _L2_gnn_ref(x, adj, W, a, gamma, beta):
        import jax, jax.numpy as jnp
        import numpy as np
        N = 2048
        IN_F = 128
        OUT_F = 128
        HEADS = 4
        HEAD_DIM = OUT_F // HEADS
        ALPHA = 0.2
        NEG_INF = -9000000000000000.0
        LN_EPS = 1e-05
        n = x.shape[0]
        h = (x @ W).reshape(n, HEADS, HEAD_DIM)
        a1 = a[:HEAD_DIM, 0]
        a2 = a[HEAD_DIM:, 0]
        s = jnp.einsum('nhd,d->nh', h, a1) + jnp.einsum('nhd,d->nh', h, a2)
        s = jnp.where(s >= 0, s, ALPHA * s)
        e = jnp.broadcast_to(s[:, :, None], (n, HEADS, n))
        mask = adj[:, None, :] > 0
        e = jnp.where(mask, e, NEG_INF)
        attn = jax.nn.softmax(e, axis=-1)
        h_prime = jnp.einsum('ihj,jhd->ihd', attn, h).reshape(n, OUT_F)
        mu = jnp.mean(h_prime, axis=-1, keepdims=True)
        var = jnp.var(h_prime, axis=-1, keepdims=True)
        out = (h_prime - mu) * jax.lax.rsqrt(var + LN_EPS) * gamma + beta
        return out

    def _L2_ffn_ref(x, weight, bias):
        import jax, jax.numpy as jnp
        import numpy as np
        IN_CH = 128
        OUT_CH = 128
        return jnp.einsum('bsi,oi->bso', x, weight) + bias

    def _L3_gnn_ref(h, adj, W, a):
        import jax, jax.numpy as jnp
        import numpy as np
        ALPHA = 0.2
        NEG_INF = -9000000000000000.0
        N, F_IN, F_OUT = (4096, 128, 128)
        Wh = h @ W
        a1, a2 = (a[:F_OUT, 0], a[F_OUT:, 0])
        f1 = Wh @ a1
        f2 = Wh @ a2
        e = jax.nn.leaky_relu(f1[:, None] + f2[None, :], negative_slope=ALPHA)
        e = jnp.where(adj > 0, e, NEG_INF)
        attention = jax.nn.softmax(e, axis=1)
        h_prime = attention @ Wh
        return jax.nn.elu(h_prime)

    def _L3_ffn_ref(x, gate_w, gate_b, w1, w2, w3):
        import jax, jax.numpy as jnp
        import numpy as np
        D_MODEL = 128
        N_EXPERTS = 16
        HIDDEN = 256
        SCALE = 0.02
        n_experts = w1.shape[0]
        logits = jnp.einsum('bsd,de->bse', x, gate_w) + gate_b
        probs = jax.nn.softmax(logits, axis=-1)
        top_probs, top_idx = jax.lax.top_k(probs, 2)
        top_probs = top_probs / jnp.sum(top_probs, axis=-1, keepdims=True)
        dispatch = jnp.sum(jax.nn.one_hot(top_idx, n_experts, dtype=x.dtype) * top_probs[..., None], axis=-2)
        h1 = jnp.einsum('bsd,edh->bseh', x, w1)
        h2 = jnp.einsum('bsd,edh->bseh', x, w2)
        hidden = jax.nn.silu(h1) * h2
        expert_out = jnp.einsum('bseh,eho->bseo', hidden, w3)
        return jnp.einsum('bseo,bse->bso', expert_out, dispatch)
    x = x + _L0_gnn_ref(_layernorm(x, axis=-1), adj, L0_gnn_W, L0_gnn_a)
    x = x + _L0_ffn_ref(_layernorm(x, axis=-1)[None], L0_ffn_Wg, L0_ffn_bg, L0_ffn_bias, L0_ffn_W1, L0_ffn_b1, L0_ffn_W2, L0_ffn_b2)[0]
    x = x + _L1_gnn_ref(_layernorm(x, axis=-1), adj, L1_gnn_W0, L1_gnn_W1, L1_gnn_a1, L1_gnn_W2, L1_gnn_a2, L1_gnn_W3, L1_gnn_a3)
    x = x + _L1_ffn_ref(_layernorm(x, axis=-1)[None], L1_ffn_router_w1, L1_ffn_router_b1, L1_ffn_router_w2, L1_ffn_router_b2, L1_ffn_expert_w1, L1_ffn_expert_b1, L1_ffn_expert_w2, L1_ffn_expert_b2, L1_ffn_expert_w3, L1_ffn_expert_b3)[0]
    x = x + _L2_gnn_ref(_layernorm(x, axis=-1), adj, L2_gnn_W, L2_gnn_a, L2_gnn_gamma, L2_gnn_beta)
    x = x + _L2_ffn_ref(_layernorm(x, axis=-1)[None], L2_ffn_weight, L2_ffn_bias)[0]
    x = x + _L3_gnn_ref(_layernorm(x, axis=-1), adj, L3_gnn_W, L3_gnn_a)
    x = x + _L3_ffn_ref(_layernorm(x, axis=-1)[None], L3_ffn_gate_w, L3_ffn_gate_b, L3_ffn_w1, L3_ffn_w2, L3_ffn_w3)[0]
    return x

_drawn_inputs = setup_inputs


def setup_inputs(seed=0):
    import zlib

    import numpy as np

    out = dict(_drawn_inputs(seed))
    spreads = {'L0_ffn_bias': (0.0, 0.275),
     'L1_ffn_router_b1': (0.0, 0.1),
     'L1_ffn_router_b2': (0.0, 0.3),
     'L1_ffn_expert_b1': (0.0, 0.8),
     'L1_ffn_expert_b2': (0.0, 0.367),
     'L1_ffn_expert_b3': (0.0, 0.1),
     'L2_gnn_gamma': (1.0, 0.2),
     'L2_gnn_beta': (0.0, 0.1),
     'L3_ffn_gate_b': (0.0, 0.8)}
    factors = {'L0_ffn_bg': 7.373,
     'L0_ffn_b1': 8.0,
     'L3_ffn_gate_w': 8.0,
     'L3_ffn_w1': 8.0,
     'L3_ffn_w2': 8.0,
     'L3_ffn_w3': 8.0}
    for name, (base, spread) in spreads.items():
        noise = np.random.default_rng([zlib.crc32(name.encode()), seed]).standard_normal(out[name].shape)
        drawn = base * np.exp(spread * noise) if base else spread * noise
        out[name] = jnp.asarray(drawn.astype(out[name].dtype))
    for name, factor in factors.items():
        out[name] = (out[name] * factor).astype(out[name].dtype)
    return out
```

```python
from contextlib import ExitStack

import concourse.bass as bass
from concourse import mybir

F32 = mybir.dt.float32
BF16 = mybir.dt.bfloat16
I32 = mybir.dt.int32
U32 = mybir.dt.uint32
ALU = mybir.AluOpType
ACT = mybir.ActivationFunctionType
AX_X = mybir.AxisListType.X

P = 128
D = 128
LN_EPS = 1e-5
BANK = 512
AW = D + 2
SLOTS = 3

GATS = [("G0", 0.2), ("G1a", 0.01), ("G1b", 0.01), ("G1c", 0.01), ("G2", None), ("G3", 0.2)]
SCORED = [g for g, (_, alpha) in enumerate(GATS) if alpha is not None]
MOES = [(8, "relu"), (6, "relu2"), (16, "silu")]
BIAS_AT = 768
UNITS = 6


def build(nc, io):
    N = io["x"].shape[0]
    NT = -(-N // P)
    NP = NT * P
    LAST = N - (NT - 1) * P
    CHUNKS = [(c, min(BANK, NP - c)) for c in range(0, NP, BANK)]
    NCH = len(CHUNKS)
    GROUPS = [(b, b * SLOTS, min(SLOTS, NT - b * SLOTS)) for b in range(-(-NT // SLOTS))]
    NG = len(GROUPS)
    TPB = BANK // P
    assert NT % 2 == 1 and LAST < P

    EXPERTS_BEFORE = [sum(e for e, _ in MOES[:f]) for f in range(len(MOES))]

    with ExitStack() as ctx:
        def sb(name, shape, dt=F32):
            return ctx.enter_context(nc.sbuf_tensor(name, shape, dt))

        def sem(name):
            return ctx.enter_context(nc.semaphore(name))

        x = sb("x", [P, NT, D])
        xn = sb("xn", [P, NT, D])
        inT = sb("inT", [P, NP])
        maskT = sb("maskT", [P, NT, NP], BF16)
        adj_i = [sb(f"adj_i{b}", [P, N], I32) for b in range(2)]
        mask_nat = [sb(f"mask_nat{b}", [P, NP], BF16) for b in range(2)]
        count_junk = sb("count_junk", [P, N], BF16)
        degree = sb("degree", [P, NT])
        ident = sb("ident", [P, P])
        ident_h = sb("ident_h", [P, P], BF16)
        ones = sb("ones", [P, P])
        real = sb("real", [P, NT])
        count = sb("count", [P, NT])
        minus_half = sb("minus_half", [P, NT])
        iota_e = sb("iota_e", [P, 16])

        stats = sb("stats", [P, NT, 6])
        moments = sb("moments", [P, NT, 2])
        var_eps = sb("var_eps", [P, NT])
        rstd = sb("rstd", [P, NT])

        w_ext = sb("w_ext", [P, len(GATS), D + 1])
        a_row = [[sb(f"a_row{g}_{h}", [P, D]) for h in range(2)] for g in range(len(GATS))]
        wa = sb("wa", [P, len(GATS), 2])
        wa_rep = [[sb(f"wa_rep{g}_{h}", [P, P]) for h in range(2)] for g in range(len(GATS))]
        dot_junk = sb("dot_junk", [P, D])
        w0 = sb("w0", [P, D])
        wh = sb("wh", [P, NT, AW])
        f2_max = sb("f2_max", [P, 1])
        f2_shift = sb("f2_shift", [P, NT])
        f2_alpha = sb("f2_alpha", [P, NT])
        f2_exp = sb("f2_exp", [P, NT])
        f1_pos = sb("f1_pos", [P, NP])
        low = [sb(f"low{b}", [P, NP]) for b in range(2)]
        prob = [sb(f"prob{b}", [P, NP]) for b in range(2)]
        inv_sum = sb("inv_sum", [P, NT])
        hp = sb("hp", [P, NT, D])
        hp_exp = sb("hp_exp", [P, NT, D])

        gate_w = [sb("gate_w0", [P, 8]), sb("gate_w1", [64, 6]), sb("gate_w2", [P, 16])]
        gate_b = [sb(f"gate_b{f}", [P, e]) for f, (e, _) in enumerate(MOES)]
        gate_b_more = sb("gate_b_more", [P, 8])
        router_w1 = sb("router_w1", [P, 64])
        router_b1 = sb("router_b1", [64, 1])
        router_h = sb("router_h", [64, NP])
        logits = sb("logits", [P, NT, 16])
        route_exp = sb("route_exp", [P, NT, 16])
        route_sum = sb("route_sum", [P, NT])
        top = sb("top", [P, NT, 8])
        top_at = sb("top_at", [P, NT, 8], U32)
        top_at_f = sb("top_at_f", [P, NT, 8])
        top_w = sb("top_w", [P, NT, 4])
        disp = sb("disp", [P, NT, 16])
        disp_2 = sb("disp_2", [P, NT, 16])
        dispT = sb("dispT", [8, NP])
        bias_out = [sb("bias_out0", [8, D]), sb("bias_out1", [6, D])]
        w_exp = [sb(f"w_exp{b}", [P, BIAS_AT + 2]) for b in range(2)]
        hid_1 = [sb(f"hid_1{b}", [P, NP]) for b in range(2)]
        hid = [sb(f"hid{b}", [P, 2, NP]) for b in range(2)]
        silu = [sb(f"silu{b}", [P, BANK]) for b in range(2)]
        lin_wT = sb("lin_wT", [P, D])
        lin_b = sb("lin_b", [P, D])
        gamma = sb("gamma", [P, D])
        beta = sb("beta", [P, D])

        ps = ctx.enter_context(nc.psum_tensor("ps", [P, 8, BANK], F32))
        TILE_BANKS, ROW_BANKS, MISC = 0, 4, 7

        def tiles_in(bank, n, width):
            return ps[:, bank, 0:n * width].rearrange("p (s w) -> p s w", w=width)

        def row_bank(c):
            return ps[:, ROW_BANKS + c, 0:CHUNKS[c][1]]

        def tile_out(t):
            return ps[:, t // TPB, (t % TPB) * P:(t % TPB + 1) * P]

        def cols(t):
            return slice(t * P, (t + 1) * P)

        x_in = sem("x_in")
        adj_in = [sem(f"adj_in{b}") for b in range(2)]
        params_in = sem("params_in")
        experts_in = [sem(f"experts_in{b}") for b in range(2)]
        out_stored = sem("out_stored")
        pool_made = sem("pool_made")
        consts_made = sem("consts_made")
        dve_done = sem("dve_done")
        act_done = sem("act_done")
        pad_cleared = sem("pad_cleared")
        adj_used = sem("adj_used")
        mask_made = sem("mask_made")
        degree_made = sem("degree_made")
        mask_turned = sem("mask_turned")
        mask_copied = sem("mask_copied")
        weights_made = sem("weights_made")
        var_made = sem("var_made")
        rstd_made = sem("rstd_made")
        xn_made = sem("xn_made")
        rows_made = sem("rows_made")
        inT_made = sem("inT_made")
        sum_made = sem("sum_made")
        f2_made = sem("f2_made")
        f2_max_made = sem("f2_max_made")
        f1_made = sem("f1_made")
        f1_read = sem("f1_read")
        wh_made = sem("wh_made")
        wh_copied = sem("wh_copied")
        f2_shifted = sem("f2_shifted")
        f2_exp_made = sem("f2_exp_made")
        low_made = sem("low_made")
        prob_made = sem("prob_made")
        prob_used = sem("prob_used")
        att_made = sem("att_made")
        hp_made = sem("hp_made")
        hp_exp_made = sem("hp_exp_made")
        router_rows = sem("router_rows")
        router_h_made = sem("router_h_made")
        logits_made = sem("logits_made")
        logits_read = sem("logits_read")
        top_diff_made = sem("top_diff_made")
        top_exp_made = sem("top_exp_made")
        disp_made = sem("disp_made")
        disp_turned = sem("disp_turned")
        dispT_made = sem("dispT_made")
        bias_made = sem("bias_made")
        bias_added = sem("bias_added")
        unit_made = sem("unit_made")
        silu_made = sem("silu_made")
        hid_made = sem("hid_made")
        y_made = sem("y_made")
        y_used = sem("y_used")
        expert_used = sem("expert_used")
        lin_made = sem("lin_made")

        INPUTS = {name: i for i, name in enumerate(
            ["G0", "F0", "G1n", "G1a", "G1b", "G1c", "F1", "G2", "F2", "G3", "F3"])}
        TOKENS = {name: i for i, name in enumerate(
            ["G0", "F0", "G1n", "G1b", "G1c", "F1", "G2", "F2", "G3", "F3"])}
        NORMS = len(TOKENS) - 2 + 1

        GAT_PARAMS = [("L0_gnn_W", "L0_gnn_a"), ("L1_gnn_W1", "L1_gnn_a1"), ("L1_gnn_W2", "L1_gnn_a2"),
                      ("L1_gnn_W3", "L1_gnn_a3"), ("L2_gnn_W", None), ("L3_gnn_W", "L3_gnn_a")]

        def row(name, lo, hi):
            ap = io[name]
            flat = ap.rearrange("a b -> (a b)") if len(ap.shape) == 2 else ap
            return flat[lo:hi].rearrange("(o n) -> o n", o=1).to_broadcast([P, hi - lo])

        param_loads = []
        for g, (w, a) in enumerate(GAT_PARAMS):
            param_loads.append((w_ext[:, g, 0:D], io[w]))
            if a:
                param_loads.append((a_row[g][0][:], row(a, 0, D)))
                param_loads.append((a_row[g][1][:], row(a, D, 2 * D)))
        param_loads += [
            (w0[:], io["L1_gnn_W0"]),
            (gate_w[0][:], io["L0_ffn_Wg"]), (gate_w[1][:], io["L1_ffn_router_w2"]),
            (gate_w[2][:], io["L3_ffn_gate_w"]),
            (gate_b[0][:], row("L0_ffn_bg", 0, 8)), (gate_b_more[:], row("L0_ffn_bias", 0, 8)),
            (gate_b[1][:], row("L1_ffn_router_b2", 0, 6)), (gate_b[2][:], row("L3_ffn_gate_b", 0, 16)),
            (router_w1[:], io["L1_ffn_router_w1"]),
            (router_b1[:], io["L1_ffn_router_b1"].rearrange("(p o) -> p o", o=1)),
            (bias_out[0][:], io["L0_ffn_b2"]), (bias_out[1][:], io["L1_ffn_expert_b3"]),
            (lin_wT[:], io["L2_ffn_weight"]), (lin_b[:], row("L2_ffn_bias", 0, D)),
            (gamma[:], row("L2_gnn_gamma", 0, D)), (beta[:], row("L2_gnn_beta", 0, D)),
        ]
        PARAMS = 16 * len(param_loads)
        X_LOADS = 32

        def expert_loads(f, e, b):
            if f == 0:
                return [(w_exp[b][:, 0:256], io["L0_ffn_W1"][bass.ds(e, 1)].rearrange("e p n -> (e p) n")),
                        (w_exp[b][:, 256:512].rearrange("p (c n) -> p c n", c=2),
                         io["L0_ffn_W2"][bass.ds(e, 1)].rearrange("e (c p) n -> (e p) c n", c=2)),
                        (w_exp[b][:, BIAS_AT:BIAS_AT + 2], io["L0_ffn_b1"][bass.ds(e, 1)].rearrange("e p n -> (e p) n"))]
            if f == 1:
                return [(w_exp[b][:, i * P:(i + 1) * P],
                         io[f"L1_ffn_expert_w{i + 1}"][bass.ds(e, 1)].rearrange("e p n -> (e p) n")) for i in range(3)] + [
                    (w_exp[b][:, BIAS_AT:BIAS_AT + 2], io["L1_ffn_expert_b12"][bass.ds(e, 1)].rearrange("e p n -> (e p) n"))]
            return [(w_exp[b][:, 0:256], io["L3_ffn_w1"][bass.ds(e, 1)].rearrange("e p n -> (e p) n")),
                    (w_exp[b][:, 256:512], io["L3_ffn_w2"][bass.ds(e, 1)].rearrange("e p n -> (e p) n")),
                    (w_exp[b][:, 512:768].rearrange("p (c n) -> p c n", c=2),
                     io["L3_ffn_w3"][bass.ds(e, 1)].rearrange("e (c p) n -> (e p) c n", c=2))]

        LOADS = [3, 4, 3]
        LOADED_BEFORE = [sum(16 * LOADS[q] * (MOES[q][0] // 2) for q in range(f)) for f in range(len(MOES))]

        block = ctx.enter_context(nc.Block())

        @block.sync
        def _(sp):
            sp.dma_start(x[:, 0:NT - 1, :], io["x"][0:(NT - 1) * P, :].rearrange("(t p) d -> p t d", p=P)).then_inc(x_in, 16)
            sp.wait_ge(pad_cleared, 1)
            sp.dma_start(x[0:LAST, NT - 1, :], io["x"][(NT - 1) * P:N, :]).then_inc(x_in, 16)
            for t in range(NT):
                rows = P if t < NT - 1 else LAST
                if t >= 2:
                    sp.wait_ge(adj_used, t - 1)
                if t == NT - 1:
                    sp.wait_ge(pad_cleared, 2)
                sp.dma_start(adj_i[t % 2][0:rows, :], io["adj"][t * P:t * P + rows, :]).then_inc(adj_in[t % 2], 16)
            for f, (E, _) in enumerate(MOES):
                def load(e, b):
                    sp.wait_ge(expert_used, EXPERTS_BEFORE[f] + e - 1)
                    for dst, src in expert_loads(f, e, b):
                        sp.dma_start(dst, src).then_inc(experts_in[b], 16)
                for b in range(2):
                    if f > 0:
                        sp.wait_ge(expert_used, EXPERTS_BEFORE[f] + b - 1)
                    for dst, src in expert_loads(f, b, b):
                        sp.dma_start(dst, src).then_inc(experts_in[b], 16)
                with sp.Fori(1, E // 2) as k:
                    for b in range(2):
                        load(2 * k + b, b)
            sp.wait_ge(y_used, sum(e for e, _ in MOES))
            sp.dma_start(io["out"][0:(NT - 1) * P, :].rearrange("(t p) d -> p t d", p=P), x[:, 0:NT - 1, :]).then_inc(out_stored, 16)
            sp.dma_start(io["out"][(NT - 1) * P:N, :], x[0:LAST, NT - 1, :]).then_inc(out_stored, 16)
            sp.wait_ge(out_stored, 32)

        @block.gpsimd
        def _(pool):
            made = 0

            def link(ins):
                nonlocal made
                made += 1
                ins.then_inc(pool_made, 1)
                pool.wait_ge(pool_made, made)

            pool.memset(ident[:], 0.0)
            pool.memset(ident_h[:], 0.0)
            pool.memset(real[:], 1.0)
            pool.memset(count[:], 1.0)
            pool.memset(minus_half[:], -0.5)
            link(pool.memset(ones[:], 1.0))
            pool.affine_select(out=ident[:], in_=ident[:], compare_op=ALU.not_equal, fill=1.0, base=0,
                               pattern=[[-1, P]], channel_multiplier=1)
            pool.affine_select(out=ident_h[:], in_=ident_h[:], compare_op=ALU.not_equal, fill=1.0, base=0,
                               pattern=[[-1, P]], channel_multiplier=1)
            pool.affine_select(out=real[:], in_=real[:], compare_op=ALU.is_gt, fill=0.0, base=N,
                               pattern=[[-P, NT]], channel_multiplier=-1)
            pool.affine_select(out=count[:], in_=count[:], compare_op=ALU.not_equal, fill=float(N), base=-N,
                               pattern=[[P, NT]], channel_multiplier=1)
            pool.iota(iota_e[:], pattern=[[1, 16]], base=0, channel_multiplier=0,
                      allow_small_or_imprecise_dtypes=True).then_inc(consts_made, 1)
            for dst, src in param_loads:
                pool.dma_start(dst, src).then_inc(params_in, 16)

            def rsqrt(n):
                pool.wait_ge(var_made, n)
                pool.tensor_tensor(rstd[:], var_eps[:], minus_half[:], ALU.pow).then_inc(rstd_made, 1)

            for n in range(NORMS):
                rsqrt(n + 1)

        @block.tensor
        def _(pe):
            def turn_masks():
                for t in range(NT):
                    half = 2 * (t % 2)
                    pe.wait_ge(mask_made, t + 1)
                    if t >= 2:
                        pe.wait_ge(mask_copied, t - 1)
                    out = ps[:, half:half + 2, :].rearrange("p b n -> p (b n)").bitcast(BF16)
                    for j in range(NT):
                        m = pe.transpose(out[:, cols(j)], mask_nat[t % 2][:, cols(j)], ident_h[:])
                    m.then_inc(mask_turned, 1)

            def rows_from_tiles(tiles):
                for c, (c0, w) in enumerate(CHUNKS):
                    for t in range(c0 // P, (c0 + w) // P):
                        m = pe.transpose(ps[:, ROW_BANKS + c, (t % TPB) * P:(t % TPB + 1) * P], tiles[:, t, :], ident[:])
                    m.then_inc(rows_made, 1)

            def normed_rows(name):
                pe.wait_ge(xn_made, TOKENS[name] + 1)
                rows_from_tiles(xn)

            def wait_input(name):
                pe.wait_ge(inT_made, NCH * (INPUTS[name] + 1))

            def attention(g):
                name, alpha = GATS[g]
                wait_input(name)
                a = SCORED.index(g) if alpha is not None else None
                if alpha is not None:
                    for c, (c0, w) in enumerate(CHUNKS):
                        w = min(w, N - c0)
                        m = pe.matmul(ps[:, ROW_BANKS + c, 0:w], wa_rep[g][1][:], inT[:, c0:c0 + w], start=True, stop=True)
                    m.then_inc(f2_made, 1)
                pe.wait_ge(sum_made, g + 1)
                for b, t0, n in GROUPS:
                    for t in range(t0, t0 + n):
                        m = pe.matmul(ps[:, b, (t - t0) * AW:(t - t0) * AW + D + 1], inT[:, cols(t)], w_ext[:, g, :],
                                      start=True, stop=True)
                    m.then_inc(wh_made, 1)
                if alpha is not None:
                    pe.wait_ge(f2_max_made, a + 1)
                    for c, (c0, w) in enumerate(CHUNKS):
                        m = pe.matmul(row_bank(c), wa_rep[g][0][:], inT[:, c0:c0 + w], start=True, stop=True)
                    m.then_inc(f1_made, 1)
                pe.wait_ge(wh_copied, NG * (g + 1))

                def neighbours(j, b, first=False, last=False):
                    pe.wait_ge(prob_made, NT * g + 1 + j)
                    for bank, t0, n in GROUPS:
                        for t in range(t0, t0 + n):
                            m = pe.matmul(ps[:, bank, (t - t0) * AW:(t - t0 + 1) * AW], prob[b][:, cols(t)],
                                          wh[:, bass.ds(j, 1), :].rearrange("p o n -> p (o n)"),
                                          start=first and t == t0, stop=last, skip_group_check=True)
                        if last and bank < NG - 1:
                            m.then_inc(att_made, 1)
                    m.then_inc(att_made if last else prob_used, 1)

                neighbours(0, 0, first=True)
                with pe.Fori(0, (NT - 3) // 2) as k:
                    neighbours(2 * k + 1, 1)
                    neighbours(2 * k + 2, 0)
                neighbours(NT - 2, 1)
                neighbours(NT - 1, 0, last=True)

            def mixture(f):
                E, kind = MOES[f]
                base = EXPERTS_BEFORE[f]
                wait_input(f"F{[0, 1, 3][f]}")
                if kind == "relu2":
                    for c, (c0, w) in enumerate(CHUNKS):
                        m = pe.matmul(ps[0:64, ROW_BANKS + c, 0:w], router_w1[:], inT[:, c0:c0 + w], start=True, stop=True)
                    m.then_inc(router_rows, 1)
                    pe.wait_ge(router_h_made, 1)
                src = router_h if kind == "relu2" else inT
                for t in range(NT):
                    m = pe.matmul(ps[:, MISC, t * E:(t + 1) * E], src[:, cols(t)], gate_w[f][:], start=True, stop=True)
                m.then_inc(logits_made, 1)

                per_load = 16 * LOADS[f]

                def unit(e, u, banks):
                    half, c = divmod(u, NCH)
                    c0, w = CHUNKS[c]
                    b = banks[0]
                    if kind == "relu":
                        m = pe.matmul(ps[:, b, 0:w], w_exp[e[1]][:, half * P:(half + 1) * P], inT[:, c0:c0 + w],
                                      start=True, stop=True)
                    elif kind == "relu2":
                        rhs = inT[:, c0:c0 + w] if half == 0 else hid_1[e[1]][:, c0:c0 + w]
                        if half == 1:
                            pe.wait_ge(hid_made, UNITS * (base + e[0]) + c + 1)
                        m = pe.matmul(ps[:, b, 0:w], w_exp[e[1]][:, half * P:(half + 1) * P], rhs, start=True, stop=True)
                    else:
                        for q in range(2):
                            m = pe.matmul(ps[:, banks[q], 0:w],
                                          w_exp[e[1]][:, q * 256 + half * P:q * 256 + (half + 1) * P],
                                          inT[:, c0:c0 + w], start=True, stop=True)
                    m.then_inc(unit_made, 1)

                ring = 2 if kind == "silu" else 4

                def hidden(e, b, k, first=False):
                    pe.wait_ge(experts_in[b], LOADED_BEFORE[f] + per_load * (k + 1))
                    for u in range(UNITS):
                        n = UNITS * b + u
                        if not (first and u < ring):
                            pe.wait_ge(hid_made, UNITS * (base + e) + u - ring + 1)
                        s = n % ring
                        unit((e, b), u, (3 + 2 * s, 4 + 2 * s) if kind == "silu" else (3 + s,))

                def output(e, b, first=False):
                    pe.wait_ge(hid_made, UNITS * (base + e + 1))
                    if not first:
                        pe.wait_ge(y_used, base + e)
                    elif f < 2:
                        pe.wait_ge(bias_added, f + 1)
                    for c, (c0, w) in enumerate(CHUNKS):
                        for t in range(c0 // P, (c0 + w) // P):
                            if kind == "relu2":
                                m = pe.matmul(tile_out(t), hid[b][:, 0, cols(t)], w_exp[b][:, 256:384], start=True, stop=True)
                            else:
                                at = 256 if kind == "relu" else 512
                                for half in range(2):
                                    m = pe.matmul(tile_out(t), hid[b][:, half, cols(t)],
                                                  w_exp[b][:, at + half * P:at + (half + 1) * P],
                                                  start=half == 0, stop=half == 1)
                        m.then_inc(y_made if c < NCH - 1 else expert_used, 1)

                hidden(0, 0, 0, first=True)
                pe.wait_ge(disp_made, f + 1)
                if f < 2:
                    for c, (c0, w) in enumerate(CHUNKS):
                        for t in range(c0 // P, (c0 + w) // P):
                            m = pe.transpose(ps[0:E, c, (t % TPB) * P:(t % TPB + 1) * P], disp[:, t, 0:E], ident[:])
                    m.then_inc(disp_turned, 1)
                    pe.wait_ge(dispT_made, f + 1)
                    for t in range(NT):
                        m = pe.matmul(tile_out(t), dispT[0:E, cols(t)], bias_out[f][:], start=True, stop=True)
                    m.then_inc(bias_made, 1)
                hidden(1, 1, 0)
                output(0, 0, first=True)
                with pe.Fori(1, E // 2) as k:
                    hidden(2 * k, 0, k)
                    output(2 * k - 1, 1)
                    hidden(2 * k + 1, 1, k)
                    output(2 * k, 0)
                output(E - 1, 1)

            pe.wait_ge(consts_made, 1)
            normed_rows("G0")
            turn_masks()
            pe.wait_ge(weights_made, 1)
            pe.wait_ge(mask_copied, NT)
            attention(0)
            normed_rows("F0")
            mixture(0)
            normed_rows("G1n")
            wait_input("G1n")
            for c, (c0, w) in enumerate(CHUNKS):
                pe.matmul(row_bank(c), w0[:], inT[:, c0:c0 + w], start=True, stop=True).then_inc(rows_made, 1)
            attention(1)
            for g, name in ((2, "G1b"), (3, "G1c")):
                pe.wait_ge(xn_made, TOKENS[name] + 1)
                rows_from_tiles(hp)
                attention(g)
            normed_rows("F1")
            mixture(1)
            normed_rows("G2")
            attention(4)
            normed_rows("F2")
            wait_input("F2")
            for t in range(NT):
                m = pe.matmul(tile_out(t), inT[:, cols(t)], lin_wT[:], start=True, stop=True)
            m.then_inc(lin_made, 1)
            normed_rows("G3")
            attention(5)
            normed_rows("F3")
            mixture(2)

        @block.scalar
        def _(act):
            chain = 0

            def copy_rows(name):
                for c, (c0, w) in enumerate(CHUNKS):
                    act.wait_ge(rows_made, NCH * INPUTS[name] + c + 1)
                    act.activation(inT[:, c0:c0 + w], row_bank(c), ACT.Copy).then_inc(inT_made, 1)

            def attention(g):
                _, alpha = GATS[g]
                for b, t0, n in GROUPS:
                    act.wait_ge(wh_made, NG * g + b + 1)
                    act.activation(wh[:, t0:t0 + n, 0:D + 1], tiles_in(b, n, AW)[:, :, 0:D + 1], ACT.Copy).then_inc(wh_copied, 1)
                if alpha is not None:
                    a = SCORED.index(g)
                    act.wait_ge(f2_shifted, a + 1)
                    act.activation(f2_exp[:], f2_shift[:], ACT.Exp).then_inc(f2_exp_made, 1)

                    def lower(j, b, first=False):
                        if not first:
                            act.wait_ge(prob_made, NT * g + j - 1)
                        act.wait_ge(f1_read, a + 1)
                        act.activation(low[b][:], f1_pos[:], ACT.Exp, bias=f2_alpha[:, bass.ds(j, 1)],
                                       scale=alpha - 1.0).then_inc(low_made, 1)

                    lower(0, 0, first=True)
                    lower(1, 1, first=True)
                    with act.Fori(1, (NT - 1) // 2) as k:
                        lower(2 * k, 0)
                        lower(2 * k + 1, 1)
                    lower(NT - 1, 0)
                    for b, t0, n in GROUPS:
                        act.wait_ge(hp_made, NG * a + b + 1)
                        act.activation(hp_exp[:, t0:t0 + n, :], hp[:, t0:t0 + n, :], ACT.Exp).then_inc(hp_exp_made, 1)

            def mixture(f):
                E, kind = MOES[f]
                base = EXPERTS_BEFORE[f]
                exps = [0, 1, 3][f]
                if kind == "relu2":
                    act.wait_ge(router_rows, 1)
                    rows = ps[0:64, ROW_BANKS:ROW_BANKS + NCH, :].rearrange("p b n -> p (b n)")[:, 0:NP]
                    act.activation(router_h[:], rows, ACT.Relu, bias=router_b1[:]).then_inc(router_h_made, 1)
                    act.wait_ge(top_diff_made, exps + 1)
                    act.activation(route_exp[:, :, 0:E], logits[:, :, 0:E], ACT.Exp)
                    act.activation(top_w[:, :, 1], top_w[:, :, 0], ACT.Exp).then_inc(top_exp_made, 1)
                    exps += 1
                act.wait_ge(top_diff_made, exps + 1)
                act.activation(top_w[:, :, 1], top_w[:, :, 0], ACT.Exp).then_inc(top_exp_made, 1)

                def units(e, b, first=False):
                    if not first:
                        act.wait_ge(expert_used, base + e - 1)
                    for u in range(UNITS):
                        half, c = divmod(u, NCH)
                        c0, w = CHUNKS[c]
                        act.wait_ge(unit_made, UNITS * (base + e) + u + 1)
                        s = (UNITS * b + u) % 4
                        if kind == "relu":
                            act.activation(hid[b][:, half, c0:c0 + w], ps[:, 3 + s, 0:w], ACT.Relu,
                                           bias=w_exp[b][:, BIAS_AT + half:BIAS_AT + half + 1]).then_inc(hid_made, 1)
                        elif kind == "relu2":
                            dst = hid[b][:, 0, c0:c0 + w] if half else hid_1[b][:, c0:c0 + w]
                            act.activation(dst, ps[:, 3 + s, 0:w], ACT.Relu,
                                           bias=w_exp[b][:, BIAS_AT + half:BIAS_AT + half + 1]).then_inc(hid_made, 1)
                        else:
                            s = u % 2
                            if not first or b or u >= 2:
                                act.wait_ge(hid_made, UNITS * (base + e) + u - 1)
                            act.activation(silu[s][:, 0:w], ps[:, 3 + 2 * s, 0:w], ACT.Silu).then_inc(silu_made, 1)

                units(0, 0, first=True)
                if f < 2:
                    act.wait_ge(disp_turned, f + 1)
                    rows = ps[0:E, 0:NCH, :].rearrange("p b n -> p (b n)")[:, 0:NP]
                    act.activation(dispT[0:E, :], rows, ACT.Copy).then_inc(dispT_made, 1)
                units(1, 1, first=True)
                with act.Fori(1, E // 2) as k:
                    units(2 * k, 0)
                    units(2 * k + 1, 1)

            copy_rows("G0")
            for t in range(NT):
                act.wait_ge(adj_used, t + 1)
                if t:
                    act.wait_ge(degree_made, t)
                act.activation(count_junk[:], mask_nat[t % 2][:, 0:N], ACT.Copy, accum_out=degree[:, t:t + 1]).then_inc(degree_made, 1)
            attention(0)
            copy_rows("F0")
            mixture(0)
            copy_rows("G1n")
            copy_rows("G1a")
            attention(1)
            copy_rows("G1b")
            attention(2)
            copy_rows("G1c")
            attention(3)
            copy_rows("F1")
            mixture(1)
            copy_rows("G2")
            attention(4)
            copy_rows("F2")
            copy_rows("G3")
            attention(5)
            copy_rows("F3")
            mixture(2)

        @block.vector
        def _(dve):
            chain = 0

            def link(ins):
                nonlocal chain
                chain += 1
                ins.then_inc(dve_done, 1)
                dve.wait_ge(dve_done, chain)

            def each(ap, n):
                return ap.unsqueeze(2).to_broadcast([P, ap.shape[1], n])

            def along_tiles(ap):
                return ap.unsqueeze(1).to_broadcast([P, NT, ap.shape[1]])

            norms = 0

            def normalise(src, dst):
                nonlocal norms
                norms += 1
                for t in range(NT):
                    ins = dve.bn_stats(stats[:, t, :], src[:, t, :])
                link(ins)
                for t in range(NT):
                    ins = dve.bn_aggr(moments[:, t, :], stats[:, t, :])
                link(ins)
                dve.tensor_scalar(var_eps[:], moments[:, :, 1], LN_EPS, None, ALU.add).then_inc(var_made, 1)
                dve.wait_ge(rstd_made, norms)
                for t in range(NT):
                    ins = dve.tensor_scalar(dst[:, t, :], src[:, t, :], moments[:, t, 0:1], rstd[:, t:t + 1],
                                            ALU.subtract, ALU.mult)
                return ins

            def attention(g):
                name, alpha = GATS[g]
                a = SCORED.index(g) if alpha is not None else None
                dve.wait_ge(inT_made, NCH * (INPUTS[name] + 1))
                dve.reduce_sum(inT[:, N:N + 1], inT[:, 0:N], AX_X).then_inc(sum_made, 1)
                rows = ps[:, ROW_BANKS:ROW_BANKS + NCH, :].rearrange("p b n -> p (b n)")
                if alpha is not None:
                    dve.wait_ge(f2_made, a + 1)
                    dve.tensor_reduce(f2_max[:], rows[:, 0:N], AX_X, ALU.max).then_inc(f2_max_made, 1)
                    dve.wait_ge(f2_max_made, a + 1)
                    dve.wait_ge(wh_copied, NG * (g + 1))
                    link(dve.scalar_tensor_tensor(f2_shift[:], wh[:, :, D], f2_max[:], real[:], ALU.subtract, ALU.mult))
                    dve.tensor_scalar(f2_alpha[:], f2_shift[:], alpha, None, ALU.mult).then_inc(f2_shifted, 1)
                    dve.wait_ge(f1_made, a + 1)
                    dve.tensor_scalar(f1_pos[:], rows[:, 0:NP], f2_max[:], 0.0, ALU.add, ALU.max).then_inc(f1_read, 1)
                    dve.wait_ge(f2_exp_made, a + 1)

                def weights(j, b, first=False):
                    if not first:
                        dve.wait_ge(prob_used, (NT - 1) * g + j - 1)
                    mask = maskT[:, bass.ds(j, 1), :].rearrange("p o n -> p (o n)")
                    if alpha is None:
                        dve.wait_ge(mask_copied, NT)
                        dve.tensor_copy(prob[b][:], mask).then_inc(prob_made, 1)
                        return
                    dve.wait_ge(low_made, NT * a + j + 1)
                    dve.scalar_tensor_tensor(prob[b][:], low[b][:], f2_exp[:, bass.ds(j, 1)], mask,
                                             ALU.max, ALU.mult).then_inc(prob_made, 1)

                weights(0, 0, first=True)
                weights(1, 1, first=True)
                with dve.Fori(1, (NT - 1) // 2) as k:
                    weights(2 * k, 0)
                    weights(2 * k + 1, 1)
                weights(NT - 1, 0)
                for b, t0, n in GROUPS:
                    dve.wait_ge(att_made, NG * g + b + 1)
                    acc = tiles_in(b, n, AW)
                    link(dve.reciprocal(inv_sum[:, t0:t0 + n], acc[:, :, D + 1]))
                    ins = dve.tensor_tensor(hp[:, t0:t0 + n, :], acc[:, :, 0:D], each(inv_sum[:, t0:t0 + n], D), ALU.mult)
                    if alpha is None:
                        link(ins)
                    else:
                        ins.then_inc(hp_made, 1)
                if alpha is None:
                    return
                for b, t0, n in GROUPS:
                    dve.wait_ge(hp_exp_made, NG * a + b + 1)
                    e = hp_exp[:, t0:t0 + n, :]
                    h = hp[:, t0:t0 + n, :]
                    link(dve.tensor_scalar(e, e, 1.0, -1.0, ALU.min, ALU.add))
                    ins = dve.tensor_tensor(h, h, e, ALU.max)
                    if name not in ("G1a", "G1b"):
                        link(ins)
                        ins = dve.tensor_tensor(x[:, t0:t0 + n, :], x[:, t0:t0 + n, :], h, ALU.add)
                        link(ins)
                if name in ("G1a", "G1b"):
                    ins.then_inc(xn_made, 1)

            def mixture(f):
                E, kind = MOES[f]
                base = EXPERTS_BEFORE[f]
                exps = [0, 1, 3][f]
                lg = logits[:, :, 0:E]
                wide = max(E, 8)
                dve.wait_ge(logits_made, f + 1)
                if wide > E:
                    dve.memset(logits[:, :, E:wide], -1e30)
                link(dve.tensor_tensor(lg, tiles_in(MISC, NT, E), along_tiles(gate_b[f][:]), ALU.add))
                if f == 0:
                    link(dve.tensor_tensor(lg, lg, along_tiles(gate_b_more[:]), ALU.add))
                for t in range(NT):
                    ins = dve.max(top[:, t, :], logits[:, t, 0:wide])
                link(ins)
                for t in range(NT):
                    ins = dve.max_index(top_at[:, t, :], top[:, t, :], logits[:, t, 0:wide])
                link(ins)
                link(dve.tensor_copy(top_at_f[:, :, 0:2], top_at[:, :, 0:2]))
                if kind == "relu2":
                    link(dve.tensor_tensor(lg, lg, each(top[:, :, 0], E), ALU.subtract))
                    dve.tensor_tensor(top_w[:, :, 0], top[:, :, 1], top[:, :, 0], ALU.subtract).then_inc(top_diff_made, 1)
                    exps += 1
                    dve.wait_ge(top_exp_made, exps)
                    link(dve.reduce_sum(route_sum[:], route_exp[:, :, 0:E], AX_X))
                    link(dve.reciprocal(top_w[:, :, 2], route_sum[:]))
                    link(dve.tensor_scalar(top_w[:, :, 1], top_w[:, :, 1], -1.0, None, ALU.add))
                    dve.tensor_tensor(top_w[:, :, 0], top_w[:, :, 1], top_w[:, :, 2], ALU.mult).then_inc(top_diff_made, 1)
                else:
                    dve.tensor_tensor(top_w[:, :, 0], top[:, :, 1], top[:, :, 0], ALU.subtract).then_inc(top_diff_made, 1)
                dve.wait_ge(top_exp_made, exps + 1)
                link(dve.tensor_scalar(top_w[:, :, 3], top_w[:, :, 1], 1.0, None, ALU.add))
                link(dve.reciprocal(top_w[:, :, 2], top_w[:, :, 3]))
                link(dve.tensor_tensor(top_w[:, :, 3], top_w[:, :, 1], top_w[:, :, 2], ALU.mult))
                places = along_tiles(iota_e[:, 0:E])
                for q, dst in enumerate((disp, disp_2)):
                    link(dve.tensor_tensor(dst[:, :, 0:E], places, each(top_at_f[:, :, q], E), ALU.is_equal))
                    link(dve.tensor_tensor(dst[:, :, 0:E], dst[:, :, 0:E], each(top_w[:, :, 2 + q], E), ALU.mult))
                dve.tensor_tensor(disp[:, :, 0:E], disp[:, :, 0:E], disp_2[:, :, 0:E], ALU.add).then_inc(disp_made, 1)
                dve.wait_ge(disp_made, f + 1)

                def gated(e, b):
                    if kind != "silu":
                        return
                    for u in range(UNITS):
                        half, c = divmod(u, NCH)
                        c0, w = CHUNKS[c]
                        s = u % 2
                        dve.wait_ge(silu_made, UNITS * e + u + 1)
                        dve.tensor_tensor(hid[b][:, half, c0:c0 + w], silu[s][:, 0:w], ps[:, 4 + 2 * s, 0:w],
                                          ALU.mult).then_inc(hid_made, 1)

                def combine(e, first=False):
                    if not first:
                        dve.wait_ge(y_used, base + e)
                    for c, (c0, w) in enumerate(CHUNKS):
                        if c < NCH - 1:
                            dve.wait_ge(y_made, (NCH - 1) * (base + e) + c + 1)
                        else:
                            dve.wait_ge(expert_used, base + e + 1)
                        for t in range(c0 // P, (c0 + w) // P):
                            ins = dve.scalar_tensor_tensor(x[:, t, :], tile_out(t), disp[:, t, bass.ds(e, 1)], x[:, t, :],
                                                           ALU.mult, ALU.add)
                    ins.then_inc(y_used, 1)

                gated(0, 0)
                if f < 2:
                    dve.wait_ge(bias_made, f + 1)
                    dve.tensor_tensor(x[:], x[:], ps[:, 0:NCH, :].rearrange("p b n -> p (b n)")[:, 0:NP]
                                      .rearrange("p (t d) -> p t d", d=D), ALU.add).then_inc(bias_added, 1)
                    dve.wait_ge(bias_added, f + 1)
                gated(1, 1)
                combine(0, first=True)
                with dve.Fori(1, E // 2) as k:
                    gated(2 * k, 0)
                    combine(2 * k - 1)
                    gated(2 * k + 1, 1)
                    combine(2 * k)
                combine(E - 1)
                dve.wait_ge(y_used, base + E)

            def token_input(src=None):
                normalise(x, xn).then_inc(xn_made, 1)

            link(dve.memset(x[:, NT - 1, :], 0.0))
            dve.memset(mask_nat[0][:], 0.0)
            dve.memset(mask_nat[1][:], 0.0).then_inc(pad_cleared, 1)
            dve.wait_ge(x_in, X_LOADS)
            token_input()

            def make(t):
                dve.wait_ge(adj_in[t % 2], 16 * (t // 2 + 1))
                if t >= 2:
                    dve.wait_ge(mask_turned, t - 1)
                dve.tensor_scalar(mask_nat[t % 2][:, 0:N], adj_i[t % 2][:], 0, None, ALU.is_gt).then_inc(adj_used, 1)

            def finish(t):
                dve.wait_ge(degree_made, t + 1)
                dve.tensor_scalar(mask_nat[t % 2][:, N:N + 1], degree[:, t:t + 1], 0.0, None, ALU.is_equal).then_inc(mask_made, 1)

            def copy_out(t):
                dve.wait_ge(mask_turned, t + 1)
                half = 2 * (t % 2)
                src = ps[:, half:half + 2, :].rearrange("p b n -> p (b n)").bitcast(BF16)[:, 0:NP]
                dve.tensor_copy(maskT[:, :, cols(t)], src.rearrange("p (j n) -> p j n", n=P)).then_inc(mask_copied, 1)

            for t in range(NT):
                if t == NT - 1:
                    dve.wait_ge(adj_used, NT - 2)
                    dve.memset(adj_i[t % 2][:], 0).then_inc(pad_cleared, 1)
                make(t)
                if t >= 1:
                    finish(t - 1)
                    copy_out(t - 1)
            finish(NT - 1)
            copy_out(NT - 1)

            dve.wait_ge(params_in, PARAMS)
            dve.wait_ge(consts_made, 1)
            dve.tensor_copy(wh[:, :, D + 1], count[:])
            for g in SCORED:
                for h in range(2):
                    dst = wa[:, g, h:h + 1]
                    link(dve.tensor_tensor_reduce(dot_junk[:], w_ext[:, g, 0:D], a_row[g][h][:], 1.0, 0.0,
                                                  ALU.mult, ALU.add, dst))
                    dve.tensor_scalar(wa_rep[g][h][:], ones[:], dst, None, ALU.mult)
            link(dve.memset(w_ext[:, :, D], 0.0))
            for g in SCORED:
                ins = dve.tensor_copy(w_ext[:, g, D:D + 1], wa[:, g, 1:2])
            ins.then_inc(weights_made, 1)

            attention(0)
            token_input()
            mixture(0)
            token_input()
            attention(1)
            attention(2)
            attention(3)
            token_input()
            mixture(1)
            token_input()
            attention(4)
            link(normalise(hp, hp_exp))
            link(dve.tensor_tensor(hp_exp[:], hp_exp[:], along_tiles(gamma[:]), ALU.mult))
            link(dve.tensor_tensor(hp_exp[:], hp_exp[:], along_tiles(beta[:]), ALU.add))
            link(dve.tensor_tensor(x[:], x[:], hp_exp[:], ALU.add))
            token_input()
            dve.wait_ge(lin_made, 1)
            lin_out = ps[:, 0:NCH, :].rearrange("p b n -> p (b n)")[:, 0:NP].rearrange("p (t d) -> p t d", d=D)
            link(dve.tensor_tensor(hp_exp[:], lin_out, along_tiles(lin_b[:]), ALU.add))
            link(dve.tensor_tensor(x[:], x[:], hp_exp[:], ALU.add))
            token_input()
            attention(5)
            token_input()
            mixture(2)


OUTPUT = "out"


def kernel(**inputs):
    import numpy as np
    import concourse.bacc as bacc
    from concourse.bass_utils import run_bass_kernel_spmd

    nc = bacc.Bacc("TRN2", target_bir_lowering=False, num_devices=1)
    arrays, io = {}, {}
    for name, value in inputs.items():
        if name == "L1_ffn_expert_b2":
            continue
        if name == "L2_gnn_a":
            continue
        a = np.asarray(value)
        if name == "L0_ffn_b1":
            a = a.reshape(a.shape[0], 2, P).transpose(0, 2, 1)
        elif name == "L1_ffn_expert_b1":
            name, a = "L1_ffn_expert_b12", np.stack([a, np.asarray(inputs["L1_ffn_expert_b2"])], axis=-1)
        elif name == "L2_ffn_weight":
            a = a.T
        a = np.ascontiguousarray(a)
        arrays[f"in_{name}"] = a
        io[name] = nc.dram_tensor(f"in_{name}", a.shape, mybir.dt.from_np(a.dtype), kind="ExternalInput").ap()
    io["out"] = nc.dram_tensor("out", inputs["x"].shape, F32, kind="ExternalOutput").ap()
    build(nc, io)
    result = run_bass_kernel_spmd(nc, [arrays], core_ids=[0])
    return result.results[0]["out"]
```

```python
from contextlib import ExitStack

import concourse.bass as bass
from concourse import mybir

F32 = mybir.dt.float32
F32R = mybir.dt.float32r
BF16 = mybir.dt.bfloat16
I32 = mybir.dt.int32
U32 = mybir.dt.uint32
ALU = mybir.AluOpType
ACT = mybir.ActivationFunctionType
AX_X = mybir.AxisListType.X

P = 128
D = 128
LN_EPS = 1e-5
BANK = 512
AW = D + 1
SLOTS = 3

GATS = [("G0", 0.2), ("G1a", 0.01), ("G1b", 0.01), ("G1c", 0.01), ("G2", None), ("G3", 0.2)]
SCORED = [g for g, (_, alpha) in enumerate(GATS) if alpha is not None]
MOES = [(8, "relu"), (6, "relu2"), (16, "silu")]
BIAS_AT = 768
OUT_AT, OUT_END = [256, 256, 512], [512, 384, 768]
SPLIT = [256, 128, 512]
AHEAD = 4
UNITS = 6


def build(nc, io):
    N = io["x"].shape[0]
    NT = -(-N // P)
    NP = NT * P
    LAST = N - (NT - 1) * P
    CHUNKS = [(c, min(BANK, NP - c)) for c in range(0, NP, BANK)]
    NCH = len(CHUNKS)
    GROUPS = [(b, b * SLOTS, min(SLOTS, NT - b * SLOTS)) for b in range(-(-NT // SLOTS))]
    NG = len(GROUPS)
    TPB = BANK // P
    assert NT % 2 == 1 and LAST < P

    EXPERTS_BEFORE = [sum(e for e, _ in MOES[:f]) for f in range(len(MOES))]

    with ExitStack() as ctx:
        def sb(name, shape, dt=F32):
            return ctx.enter_context(nc.sbuf_tensor(name, shape, dt))

        def sem(name):
            return ctx.enter_context(nc.semaphore(name))

        x = sb("x", [P, NT, D])
        xn = sb("xn", [P, NT, D])
        inT = sb("inT", [P, NP])
        maskT = sb("maskT", [P, NT, NP], BF16)
        degree = sb("degree", [P, NT])
        ident = sb("ident", [P, P])
        ident_h = sb("ident_h", [P, P], BF16)
        ones = sb("ones", [P, P])
        real = sb("real", [P, NT])
        count = sb("count", [P, NT])
        minus_half = sb("minus_half", [P, NT])
        iota_e = sb("iota_e", [P, 16])

        stats = sb("stats", [P, NT, 6])
        moments = sb("moments", [P, NT, 2])
        var_eps = sb("var_eps", [P, NT])
        rstd = sb("rstd", [P, NT])
        neg_mean = sb("neg_mean", [P, NT])
        shift = sb("shift", [P, NT])

        w_gat = sb("w_gat", [P, len(GATS), D])
        a_row = [sb(f"a_row{g}", [P, 2 * D]) for g in range(len(GATS))]
        wa = sb("wa", [P, len(GATS), 2])
        wa1_rep = [sb(f"wa1_rep{g}", [P, P]) for g in range(len(GATS))]
        dot_junk = sb("dot_junk", [P, D])
        w0 = sb("w0", [P, D])
        wh = sb("wh", [P, NT, AW])
        sum_parts = sb("sum_parts", [P, NCH])
        f2_top = sb("f2_top", [P, 1])
        f2_top_all = sb("f2_top_all", [1, 1])
        f2_max = sb("f2_max", [P, 1])
        f2_shift = sb("f2_shift", [P, NT])
        f2_alpha = sb("f2_alpha", [P, NT])
        f2_exp = sb("f2_exp", [P, NT])
        f1_pos = sb("f1_pos", [P, NP])
        low = [sb(f"low{b}", [P, NP]) for b in range(2)]
        prob = [sb(f"prob{b}", [P, NP]) for b in range(2)]
        adj_i = [buf[:, 0:N].bitcast(I32) for buf in low + prob]
        count_junk = f1_pos[:, 0:NP // 2].bitcast(BF16)[:, 0:N]
        inv_sum = sb("inv_sum", [P, NT])
        hp = sb("hp", [P, NT, D])
        hp_exp = sb("hp_exp", [P, NT, D])

        gate_w = [sb("gate_w0", [P, 8]), sb("gate_w1", [64, 6]), sb("gate_w2", [P, 16])]
        gate_b = [sb(f"gate_b{f}", [P, e]) for f, (e, _) in enumerate(MOES)]
        gate_b_more = sb("gate_b_more", [P, 8])
        router_w1 = sb("router_w1", [P, 64])
        router_b1 = sb("router_b1", [64, 1])
        router_h = sb("router_h", [64, NP])
        logits = sb("logits", [P, NT, 16])
        route_exp = sb("route_exp", [P, NT, 16])
        route_sum = sb("route_sum", [P, NT])
        top = sb("top", [P, NT, 8])
        top_at = sb("top_at", [P, NT, 8], U32)
        top_at_f = sb("top_at_f", [P, NT, 8])
        top_w = sb("top_w", [P, NT, 4])
        disp = sb("disp", [P, NT, 16])
        disp_2 = sb("disp_2", [P, NT, 16])
        dispT = sb("dispT", [8, NP])
        bias_out = [sb("bias_out0", [8, D]), sb("bias_out1", [6, D])]
        w_exp = [sb(f"w_exp{b}", [P, BIAS_AT + 2]) for b in range(2)]
        w_hi = [sb(f"w_hi{b}", [P, max(SPLIT)], F32R) for b in range(2)]
        w_lo = [sb(f"w_lo{b}", [P, max(SPLIT)], F32R) for b in range(2)]
        in_hi = sb("in_hi", [P, NP], F32R)
        in_lo = sb("in_lo", [P, NP], F32R)
        hid = [sb(f"hid{b}", [P, 2, NP]) for b in range(2)]
        mask_nat = [hid[q // 2][:, q % 2, :].bitcast(BF16)[:, 0:NP] for q in range(AHEAD)]
        mask_last = sb("mask_last", [P, NP], BF16)
        wh_part = [hid[0][:, h, :].bitcast(BF16)[:, 0:NT * AW].rearrange("p (t w) -> p t w", w=AW) for h in range(2)] + [
            hid[1][:, 0, :].bitcast(BF16)[:, 0:NT * AW].rearrange("p (t w) -> p t w", w=AW)]
        wh_rest = sb("wh_rest", [P, NT, AW])
        silu = [f1_pos[:, b * BANK:(b + 1) * BANK] for b in range(2)]
        lin_wT = sb("lin_wT", [P, D])
        lin_b = sb("lin_b", [1, D])
        gamma = sb("gamma", [P, D])
        beta = sb("beta", [P, D])

        ps = ctx.enter_context(nc.psum_tensor("ps", [P, 8, BANK], F32))
        TILE_BANKS, ROW_BANKS, MISC = 0, 4, 7

        def tiles_in(bank, n, width):
            return ps[:, bank, 0:n * width].rearrange("p (s w) -> p s w", w=width)

        def row_bank(c):
            return ps[:, ROW_BANKS + c, 0:CHUNKS[c][1]]

        def tile_out(t):
            return ps[:, t // TPB, (t % TPB) * P:(t % TPB + 1) * P]

        def cols(t):
            return slice(t * P, (t + 1) * P)

        x_in = sem("x_in")
        adj_in = [sem(f"adj_in{b}") for b in range(AHEAD)]
        gat_in = sem("gat_in")
        params_in = sem("params_in")
        experts_in = [sem(f"experts_in{b}") for b in range(2)]
        experts_out_in = [sem(f"experts_out_in{b}") for b in range(2)]
        out_stored = sem("out_stored")
        pool_made = sem("pool_made")
        consts_made = sem("consts_made")
        dve_done = sem("dve_done")
        act_done = sem("act_done")
        pad_cleared = sem("pad_cleared")
        mask_cleared = sem("mask_cleared")
        adj_used = sem("adj_used")
        mask_made = sem("mask_made")
        degree_made = sem("degree_made")
        mask_turned = sem("mask_turned")
        mask_copied = sem("mask_copied")
        weights_made = sem("weights_made")
        var_made = sem("var_made")
        rstd_made = sem("rstd_made")
        xn_dve = sem("xn_dve")
        xn_act = sem("xn_act")
        x_shifted = sem("x_shifted")
        elu_made = sem("elu_made")
        x_done = sem("x_done")
        rows_made = sem("rows_made")
        inT_made = sem("inT_made")
        sum_made = sem("sum_made")
        f2_made = sem("f2_made")
        f2_top_made = sem("f2_top_made")
        f2_top_turned = sem("f2_top_turned")
        f2_top_all_made = sem("f2_top_all_made")
        f2_max_spread = sem("f2_max_spread")
        f1_made = sem("f1_made")
        f1_read = sem("f1_read")
        wh_made = sem("wh_made")
        wh_copied = sem("wh_copied")
        f2_shifted = sem("f2_shifted")
        f2_exp_made = sem("f2_exp_made")
        low_made = sem("low_made")
        prob_made = sem("prob_made")
        prob_used = sem("prob_used")
        att_made = sem("att_made")
        hp_made = sem("hp_made")
        hp_exp_made = sem("hp_exp_made")
        router_rows = sem("router_rows")
        router_h_made = sem("router_h_made")
        logits_made = sem("logits_made")
        logits_read = sem("logits_read")
        top_diff_made = sem("top_diff_made")
        top_exp_made = sem("top_exp_made")
        disp_made = sem("disp_made")
        disp_turned = sem("disp_turned")
        dispT_made = sem("dispT_made")
        bias_made = sem("bias_made")
        bias_added = sem("bias_added")
        unit_made = sem("unit_made")
        silu_made = sem("silu_made")
        hid_made = sem("hid_made")
        in_w_split = sem("in_w_split")
        in_w_high = sem("in_w_high")
        in_hi_made = sem("in_hi_made")
        in_lo_made = sem("in_lo_made")
        wh_split = sem("wh_split")
        y_made = sem("y_made")
        y_used = sem("y_used")
        expert_used = sem("expert_used")
        lin_made = sem("lin_made")

        INPUTS = {name: i for i, name in enumerate(
            ["G0", "F0", "G1n", "G1a", "G1b", "G1c", "F1", "G2", "F2", "G3", "F3"])}
        NORMS = {name: i for i, name in enumerate(["G0", "F0", "G1n", "F1", "G2", "in G2", "F2", "G3", "F3"])}
        SUMMED = ("G0", "G1a", "G1b", "G1c", "G2", "G3")

        GAT_PARAMS = [("L0_gnn_W", "L0_gnn_a"), ("L1_gnn_W1", "L1_gnn_a1"), ("L1_gnn_W2", "L1_gnn_a2"),
                      ("L1_gnn_W3", "L1_gnn_a3"), ("L2_gnn_W", None), ("L3_gnn_W", "L3_gnn_a")]

        def row(name, lo, hi):
            ap = io[name]
            flat = ap.rearrange("a b -> (a b)") if len(ap.shape) == 2 else ap
            return flat[lo:hi].rearrange("(o n) -> o n", o=1).to_broadcast([P, hi - lo])

        gat_loads, param_loads = [], []
        for g, (w, a) in enumerate(GAT_PARAMS):
            gat_loads.append((w_gat[:, g, :], io[w]))
            if a:
                gat_loads.append((a_row[g][:], row(a, 0, 2 * D)))
        param_loads += [
            (w0[:], io["L1_gnn_W0"]),
            (gate_w[0][:], io["L0_ffn_Wg"]), (gate_w[1][:], io["L1_ffn_router_w2"]),
            (gate_w[2][:], io["L3_ffn_gate_w"]),
            (gate_b[0][:], row("L0_ffn_bg", 0, 8)), (gate_b_more[:], row("L0_ffn_bias", 0, 8)),
            (gate_b[1][:], row("L1_ffn_router_b2", 0, 6)), (gate_b[2][:], row("L3_ffn_gate_b", 0, 16)),
            (router_w1[:], io["L1_ffn_router_w1"]),
            (router_b1[:], io["L1_ffn_router_b1"].rearrange("(p o) -> p o", o=1)),
            (bias_out[0][:], io["L0_ffn_b2"]), (bias_out[1][:], io["L1_ffn_expert_b3"]),
            (lin_wT[:], io["L2_ffn_weight"]), (lin_b[:], io["L2_ffn_bias"].rearrange("(o n) -> o n", o=1)),
            (gamma[:], row("L2_gnn_gamma", 0, D)), (beta[:], row("L2_gnn_beta", 0, D)),
        ]
        GAT_LOADED, PARAMS = 16 * len(gat_loads), 16 * len(param_loads)

        def halves(c):
            t0, n = CHUNKS[c][0] // P, CHUNKS[c][1] // P
            return range(t0, t0 + (n + 1) // 2), range(t0 + (n + 1) // 2, t0 + n)
        X_LOADS = 32

        def expert_loads(f, e, b):
            def one(name):
                return io[name][bass.ds(e, 1)].rearrange("e p n -> (e p) n")
            biases = w_exp[b][:, BIAS_AT:BIAS_AT + 2]
            if f == 0:
                return [(w_exp[b][:, 0:256], one("L0_ffn_W1")), (biases, one("L0_ffn_b1"))]
            if f == 1:
                return [(w_exp[b][:, i * P:(i + 1) * P], one(f"L1_ffn_expert_w{i + 1}")) for i in range(2)] + [
                    (biases, one("L1_ffn_expert_b12"))]
            return [(w_exp[b][:, 0:256], one("L3_ffn_w1")), (w_exp[b][:, 256:512], one("L3_ffn_w2"))]

        def output_load(f, e, b):
            src = io[["L0_ffn_W2", "L1_ffn_expert_w3", "L3_ffn_w3"][f]][bass.ds(e, 1)]
            n = OUT_END[f] - OUT_AT[f]
            return (w_exp[b][:, OUT_AT[f]:OUT_END[f]].rearrange("p (c n) -> p c n", n=D),
                    src.rearrange("e (c p) n -> (e p) c n", c=n // D))

        LOADS = [2, 3, 2]
        LOADED_BEFORE = [sum(16 * LOADS[q] * (MOES[q][0] // 2) for q in range(f)) for f in range(len(MOES))]
        OUT_LOADED_BEFORE = [16 * EXPERTS_BEFORE[f] // 2 for f in range(len(MOES))]

        block = ctx.enter_context(nc.Block())

        @block.sync
        def _(sp):
            sp.dma_start(x[:, 0:NT - 1, :], io["x"][0:(NT - 1) * P, :].rearrange("(t p) d -> p t d", p=P)).then_inc(x_in, 16)
            sp.wait_ge(pad_cleared, 1)
            sp.dma_start(x[0:LAST, NT - 1, :], io["x"][(NT - 1) * P:N, :]).then_inc(x_in, 16)
            for t in range(NT):
                rows = P if t < NT - 1 else LAST
                if t >= AHEAD:
                    sp.wait_ge(adj_used, t - AHEAD + 1)
                sp.dma_start(adj_i[t % AHEAD][0:rows, :], io["adj"][t * P:t * P + rows, :]).then_inc(adj_in[t % AHEAD], 16)
            for f, (E, _) in enumerate(MOES):
                def load(e, b, first=False):
                    if not first or f > 0:
                        sp.wait_ge(hid_made, UNITS * (EXPERTS_BEFORE[f] + e - 1))
                    if first and f > 0:
                        sp.wait_ge(expert_used, EXPERTS_BEFORE[f] + e - 1)
                    for dst, src in expert_loads(f, e, b):
                        sp.dma_start(dst, src).then_inc(experts_in[b], 16)
                    if not first:
                        sp.wait_ge(expert_used, EXPERTS_BEFORE[f] + e - 1)
                    sp.dma_start(*output_load(f, e, b)).then_inc(experts_out_in[b], 16)
                for b in range(2):
                    load(b, b, first=True)
                with sp.Fori(1, E // 2) as k:
                    for b in range(2):
                        load(2 * k + b, b)
            for c, (c0, w) in enumerate(CHUNKS):
                sp.wait_ge(x_done, c + 1)
                full = min(w, (NT - 1) * P - c0)
                sp.dma_start(io["out"][c0:c0 + full, :].rearrange("(t p) d -> p t d", p=P),
                             x[:, c0 // P:(c0 + full) // P, :]).then_inc(out_stored, 16)
            sp.dma_start(io["out"][(NT - 1) * P:N, :], x[0:LAST, NT - 1, :]).then_inc(out_stored, 16)
            sp.wait_ge(out_stored, 16 * (NCH + 1))

        @block.gpsimd
        def _(pool):
            made = 0

            def link(ins):
                nonlocal made
                made += 1
                ins.then_inc(pool_made, 1)
                pool.wait_ge(pool_made, made)

            pool.memset(ident[:], 0.0)
            pool.memset(ident_h[:], 0.0)
            pool.memset(real[:], 1.0)
            pool.memset(count[:], 1.0)
            pool.memset(minus_half[:], -0.5)
            link(pool.memset(ones[:], 1.0))
            pool.affine_select(out=ident[:], in_=ident[:], compare_op=ALU.not_equal, fill=1.0, base=0,
                               pattern=[[-1, P]], channel_multiplier=1)
            pool.affine_select(out=ident_h[:], in_=ident_h[:], compare_op=ALU.not_equal, fill=1.0, base=0,
                               pattern=[[-1, P]], channel_multiplier=1)
            pool.affine_select(out=real[:], in_=real[:], compare_op=ALU.is_gt, fill=0.0, base=N,
                               pattern=[[-P, NT]], channel_multiplier=-1)
            pool.affine_select(out=count[:], in_=count[:], compare_op=ALU.not_equal, fill=float(N), base=-N,
                               pattern=[[P, NT]], channel_multiplier=1)
            pool.iota(iota_e[:], pattern=[[1, 16]], base=0, channel_multiplier=0,
                      allow_small_or_imprecise_dtypes=True).then_inc(consts_made, 1)
            for mask in mask_nat:
                pool.memset(mask[:, N:NP], 0.0)
            pool.memset(mask_last[:], 0.0).then_inc(mask_cleared, 1)

            def scales(name):
                for c, (c0, w) in enumerate(CHUNKS):
                    pool.wait_ge(var_made, NCH * NORMS[name] + c + 1)
                    tiles = slice(c0 // P, (c0 + w) // P)
                    link(pool.tensor_tensor(rstd[:, tiles], var_eps[:, tiles], minus_half[:, tiles], ALU.pow))
                    pool.tensor_tensor(shift[:, tiles], neg_mean[:, tiles], rstd[:, tiles], ALU.mult).then_inc(rstd_made, 1)

            def shift_x(name):
                pool.wait_ge(xn_dve, NCH * (NORMS[name] + 1))
                pool.wait_ge(xn_act, NCH * (NORMS[name] + 1))
                if name == "G2":
                    pool.tensor_tensor(x[:], x[:], beta[:].unsqueeze(1).to_broadcast([P, NT, D]), ALU.add).then_inc(x_shifted, 1)
                else:
                    pool.tensor_scalar(x[:], x[:], 1.0, -1.0, ALU.mult, ALU.add).then_inc(x_shifted, 1)

            def mixture(f):
                E, kind = MOES[f]
                base = EXPERTS_BEFORE[f]

                def low_halves(e, b):
                    pool.wait_ge(in_w_high, base + e + 1)
                    pool.tensor_tensor(w_lo[b][:, 0:SPLIT[f]], w_exp[b][:, 0:SPLIT[f]],
                                       w_hi[b][:, 0:SPLIT[f]].bitcast(F32), ALU.subtract).then_inc(in_w_split, 1)

                with pool.Fori(0, E // 2) as k:
                    low_halves(2 * k, 0)
                    low_halves(2 * k + 1, 1)

            for stage in NORMS:
                scales(stage)
                if stage == "G0":
                    for dst, src in param_loads:
                        pool.dma_start(dst, src).then_inc(params_in, 16)
                if stage in ("G0", "G1n", "G2", "G3"):
                    shift_x(stage)
                if stage in ("F0", "F1", "F3"):
                    mixture(("F0", "F1", "F3").index(stage))

        @block.tensor
        def _(pe):
            def turn_masks():
                for t in range(NT):
                    half = 2 * (t % 2)
                    pe.wait_ge(mask_made, t + 1)
                    if t >= 2:
                        pe.wait_ge(mask_copied, t - 1)
                    out = ps[:, half:half + 2, :].rearrange("p b n -> p (b n)").bitcast(BF16)
                    mask = mask_nat[t % AHEAD] if t < NT - 1 else mask_last
                    for j in range(NT):
                        m = pe.transpose(out[:, cols(j)], mask[:, cols(j)], ident_h[:])
                    m.then_inc(mask_turned, 1)

            def rows_from_tiles(tiles, wait_chunk):
                for c, (c0, w) in enumerate(CHUNKS):
                    wait_chunk(c)
                    for t in range(c0 // P, (c0 + w) // P):
                        m = pe.transpose(ps[:, ROW_BANKS + c, (t % TPB) * P:(t % TPB + 1) * P], tiles[:, t, :], ident[:])
                    m.then_inc(rows_made, 1)

            def normed_rows(name):
                def wait_chunk(c):
                    pe.wait_ge(xn_dve, NCH * NORMS[name] + c + 1)
                    pe.wait_ge(xn_act, NCH * NORMS[name] + c + 1)
                rows_from_tiles(xn, wait_chunk)

            def wait_input(name):
                pe.wait_ge(inT_made, NCH * (INPUTS[name] + 1))

            def wait_input_chunk(name, c):
                pe.wait_ge(inT_made, NCH * INPUTS[name] + c + 1)

            def attention(g):
                name, alpha = GATS[g]
                a = SCORED.index(g) if alpha is not None else None

                def f1_rows(c):
                    c0, w = CHUNKS[c]
                    wait_input_chunk(name, c)
                    pe.matmul(row_bank(c), wa1_rep[g][:], inT[:, c0:c0 + w], start=True, stop=True).then_inc(f1_made, 1)

                def node_values(b):
                    _, t0, n = GROUPS[b]
                    for t in range(t0, t0 + n):
                        m = pe.matmul(ps[:, b, (t - t0) * AW:(t - t0) * AW + D], inT[:, cols(t)], w_gat[:, g, :],
                                      start=True, stop=True)
                    m.then_inc(wh_made, 1)

                if alpha is not None:
                    for c in range(NCH - 1):
                        f1_rows(c)
                    wait_input(name)
                    pe.wait_ge(sum_made, g + 1)
                    for t in range(NT):
                        m = pe.matmul(ps[:, MISC, t:t + 1], inT[:, cols(t)], wa[:, g, 1:2], start=True, stop=True)
                    m.then_inc(f2_made, 1)
                    f1_rows(NCH - 1)
                    pe.wait_ge(f2_top_made, a + 1)
                    pe.transpose(ps[0:1, MISC, NT + 1:NT + 1 + P], f2_top[:], ident[:]).then_inc(f2_top_turned, 1)
                    node_values(0)
                    pe.wait_ge(f2_top_all_made, a + 1)
                    pe.matmul(ps[:, MISC, NT:NT + 1], ones[0:1, :], f2_top_all[:], start=True, stop=True).then_inc(f2_max_spread, 1)
                else:
                    wait_input(name)
                    pe.wait_ge(sum_made, g + 1)
                    node_values(0)
                for b in range(1, NG):
                    node_values(b)
                if alpha is None:
                    pe.wait_ge(mask_copied, NT)

                def neighbours(j, b, first=False, last=False):
                    if alpha is None:
                        left = maskT[:, bass.ds(j, 1), :].rearrange("p o n -> p (o n)")
                        rights = [part[:, bass.ds(j, 1), :].rearrange("p o n -> p (o n)") for part in wh_part]
                    else:
                        left = prob[b]
                        rights = [wh[:, bass.ds(j, 1), :].rearrange("p o n -> p (o n)")]
                        if not first:
                            pe.wait_ge(prob_made, (NCH + NT - 1) * a + NCH + j)
                    for bank, t0, n in GROUPS:
                        if first:
                            pe.wait_ge(wh_copied, NG * g + bank + 1)
                        for t in range(t0, t0 + n):
                            if first and alpha is not None and t % TPB == 0:
                                pe.wait_ge(prob_made, (NCH + NT - 1) * a + t // TPB + 1)
                            for q, right in enumerate(rights):
                                m = pe.matmul(ps[:, bank, (t - t0) * AW:(t - t0 + 1) * AW], left[:, cols(t)], right,
                                              start=first and t == t0 and q == 0, stop=last and q == len(rights) - 1,
                                              skip_group_check=True)
                        if last:
                            m.then_inc(att_made, 1)
                    if not last and alpha is not None:
                        m.then_inc(prob_used, 1)

                peeled = 1
                if alpha is None:
                    pe.wait_ge(wh_split, 5)
                neighbours(0, 0, first=True)
                if alpha is None:
                    peeled = SLOTS
                    for j in range(1, SLOTS):
                        neighbours(j, j % 2)
                    pe.wait_ge(wh_split, 10)
                with pe.Fori(0, (NT - 2 - peeled) // 2) as k:
                    neighbours(2 * k + peeled, 1)
                    neighbours(2 * k + peeled + 1, 0)
                neighbours(NT - 2, 1)
                neighbours(NT - 1, 0, last=True)

            def mixture(f):
                E, kind = MOES[f]
                base = EXPERTS_BEFORE[f]
                name = f"F{[0, 1, 3][f]}"
                if kind == "relu2":
                    for c, (c0, w) in enumerate(CHUNKS):
                        wait_input_chunk(name, c)
                        m = pe.matmul(ps[0:64, ROW_BANKS + c, 0:w], router_w1[:], inT[:, c0:c0 + w], start=True, stop=True)
                    m.then_inc(router_rows, 1)
                    pe.wait_ge(router_h_made, 1)
                src = router_h if kind == "relu2" else inT
                for t in range(NT):
                    if t % TPB == 0 and kind != "relu2":
                        wait_input_chunk(name, t // TPB)
                    m = pe.matmul(ps[:, MISC, t * E:(t + 1) * E], src[:, cols(t)], gate_w[f][:], start=True, stop=True)
                m.then_inc(logits_made, 1)

                def product(out, left, right):
                    pe.matmul(out, left[0], right[0], start=True, stop=False)
                    pe.matmul(out, left[0], right[1], start=False, stop=False)
                    return pe.matmul(out, left[1], right[0], start=False, stop=True)

                def w_cols(b, lo):
                    return w_hi[b][:, lo:lo + P], w_lo[b][:, lo:lo + P]

                ring = 2 if kind == "silu" else 4

                def units(e, b, which, first=False):
                    if 0 in which:
                        pe.wait_ge(in_w_split, base + e + 1)
                    for u in which:
                        half, c = divmod(u, NCH)
                        c0, w = CHUNKS[c]
                        if first and u < NCH:
                            pe.wait_ge(in_lo_made, NCH * f + c + 1)
                        if not (first and u < ring):
                            pe.wait_ge(hid_made, UNITS * (base + e) + u - ring + 1)
                        s = (UNITS * b + u) % ring
                        x_halves = in_hi[:, c0:c0 + w], in_lo[:, c0:c0 + w]
                        if kind == "relu2" and half == 1:
                            pe.wait_ge(hid_made, UNITS * (base + e) + c + 1)
                            m = pe.matmul(ps[:, 3 + s, 0:w], w_exp[b][:, P:2 * P], hid[b][:, 0, c0:c0 + w],
                                          start=True, stop=True)
                        elif kind == "silu":
                            product(ps[:, 3 + 2 * s, 0:w], w_cols(b, half * P), x_halves)
                            m = product(ps[:, 4 + 2 * s, 0:w], w_cols(b, 256 + half * P), x_halves)
                        else:
                            m = product(ps[:, 3 + s, 0:w], w_cols(b, half * P), x_halves)
                        m.then_inc(unit_made, 1)

                def output(e, b, k, first=False):
                    pe.wait_ge(hid_made, UNITS * (base + e + 1))
                    pe.wait_ge(experts_out_in[b], OUT_LOADED_BEFORE[f] + 16 * (k + 1))
                    if not first:
                        pe.wait_ge(y_used, base - f + e)
                    elif f < 2:
                        pe.wait_ge(bias_added, f + 1)
                    halves = (1,) if kind == "relu2" else (0, 1)
                    for c, (c0, w) in enumerate(CHUNKS):
                        for t in range(c0 // P, (c0 + w) // P):
                            for q, half in enumerate(halves):
                                m = pe.matmul(tile_out(t), hid[b][:, half, cols(t)],
                                              w_exp[b][:, OUT_AT[f] + q * P:OUT_AT[f] + (q + 1) * P],
                                              start=q == 0, stop=q == len(halves) - 1)
                        m.then_inc(y_made if c < NCH - 1 else expert_used, 1)

                def step(e, b, k, first=False):
                    if kind == "relu2":
                        units(e, b, range(0, NCH))
                        output(e - 1, 1 - b, k + b - 1, first)
                        units(e, b, range(NCH, UNITS))
                    else:
                        units(e, b, range(UNITS))
                        output(e - 1, 1 - b, k + b - 1, first)

                units(0, 0, range(UNITS), first=True)
                units(1, 1, range(NCH if kind == "relu2" else UNITS))
                if f < 2:
                    pe.wait_ge(disp_made, f + 1)
                    for c, (c0, w) in enumerate(CHUNKS):
                        for t in range(c0 // P, (c0 + w) // P):
                            m = pe.transpose(ps[0:E, c, (t % TPB) * P:(t % TPB + 1) * P], disp[:, t, 0:E], ident[:])
                    m.then_inc(disp_turned, 1)
                    pe.wait_ge(dispT_made, f + 1)
                    for t in range(NT):
                        m = pe.matmul(tile_out(t), dispT[0:E, cols(t)], bias_out[f][:], start=True, stop=True)
                    m.then_inc(bias_made, 1)
                output(0, 0, 0, first=True)
                if kind == "relu2":
                    units(1, 1, range(NCH, UNITS))
                with pe.Fori(1, E // 2) as k:
                    step(2 * k, 0, k)
                    step(2 * k + 1, 1, k)
                output(E - 1, 1, E // 2 - 1)

            pe.wait_ge(consts_made, 1)
            normed_rows("G0")
            turn_masks()
            pe.wait_ge(weights_made, 1)
            pe.wait_ge(mask_copied, NT)
            attention(0)
            normed_rows("F0")
            pe.wait_ge(params_in, PARAMS)
            mixture(0)
            normed_rows("G1n")
            for c, (c0, w) in enumerate(CHUNKS):
                wait_input_chunk("G1n", c)
                pe.matmul(row_bank(c), w0[:], inT[:, c0:c0 + w], start=True, stop=True).then_inc(rows_made, 1)
            pe.wait_ge(weights_made, 2)
            attention(1)
            for i, name in enumerate(("G1b", "G1c")):
                def wait_chunk(c):
                    tiles = sum(CHUNKS[c]) // P
                    pe.wait_ge(elu_made, NG * i + -(-tiles // SLOTS))
                rows_from_tiles(hp, wait_chunk)
                attention(2 + i)
            normed_rows("F1")
            mixture(1)
            normed_rows("G2")
            attention(4)
            pe.wait_ge(hp_made, NG * (len(SCORED) - 1 + 1))
            for t in range(NT):
                m = pe.matmul(tile_out(t), ones[0:1, :], lin_b[:], start=t % TPB == 0, stop=False, skip_group_check=True)
            normed_rows("F2")
            for t in range(NT):
                if t % TPB == 0:
                    wait_input_chunk("F2", t // TPB)
                m = pe.matmul(tile_out(t), inT[:, cols(t)], lin_wT[:], start=False, stop=True, skip_group_check=True)
                if t % TPB == TPB - 1 or t == NT - 1:
                    m.then_inc(lin_made, 1)
            normed_rows("G3")
            attention(5)
            normed_rows("F3")
            mixture(2)

        @block.scalar
        def _(act):
            chain = 0

            def copy_rows(name, chunks=range(NCH)):
                for c in chunks:
                    c0, w = CHUNKS[c]
                    act.wait_ge(rows_made, NCH * INPUTS[name] + c + 1)
                    if name not in SUMMED:
                        act.activation(inT[:, c0:c0 + w], row_bank(c), ACT.Copy).then_inc(inT_made, 1)
                        continue
                    real_w = min(w, N - c0)
                    ins = act.activation(inT[:, c0:c0 + real_w], ps[:, ROW_BANKS + c, 0:real_w], ACT.Copy,
                                         accum_out=sum_parts[:, c:c + 1])
                    if real_w < w:
                        ins = act.activation(inT[:, N + 1:c0 + w], ps[:, ROW_BANKS + c, real_w + 1:w], ACT.Copy)
                    ins.then_inc(inT_made, 1)

            def normalise(name, src, dst, c):
                act.wait_ge(rstd_made, NCH * NORMS[name] + c + 1)
                for t in halves(c)[1]:
                    ins = act.activation(dst[:, t, :], src[:, t, :], ACT.Identity, bias=shift[:, t:t + 1], scale=rstd[:, t:t + 1])
                ins.then_inc(xn_act, 1)

            def normed_rows(name):
                normalise(name, x, xn, 0)
                for c in range(1, NCH):
                    normalise(name, x, xn, c)
                    copy_rows(name, [c - 1])
                copy_rows(name, [NCH - 1])

            def attention(g):
                _, alpha = GATS[g]
                a = SCORED.index(g) if alpha is not None else None
                PROBS = NCH + NT - 1

                def copy_values(b):
                    _, t0, n = GROUPS[b]
                    act.wait_ge(wh_made, NG * g + b + 1)
                    act.activation(wh[:, t0:t0 + n, 0:D], tiles_in(b, n, AW)[:, :, 0:D], ACT.Copy).then_inc(wh_copied, 1)

                copy_values(0)
                if alpha is None:
                    for b in range(1, NG):
                        copy_values(b)
                    return
                act.wait_ge(f2_shifted, a + 1)
                act.activation(f2_exp[:], f2_shift[:], ACT.Exp).then_inc(f2_exp_made, 1)
                for c, (c0, w) in enumerate(CHUNKS):
                    act.wait_ge(f1_read, NCH * a + c + 1)
                    act.activation(low[0][:, c0:c0 + w], f1_pos[:, c0:c0 + w], ACT.Exp, bias=f2_alpha[:, 0:1],
                                   scale=alpha - 1.0).then_inc(low_made, 1)
                    copy_values(c + 1)

                def lower(j, b, first=False):
                    if not first:
                        act.wait_ge(prob_made, PROBS * a + NCH + j - 2)
                    act.activation(low[b][:], f1_pos[:], ACT.Exp, bias=f2_alpha[:, bass.ds(j, 1)],
                                   scale=alpha - 1.0).then_inc(low_made, 1)

                lower(1, 1, first=True)
                with act.Fori(1, (NT - 1) // 2) as k:
                    lower(2 * k, 0)
                    lower(2 * k + 1, 1)
                lower(NT - 1, 0)
                for b, t0, n in GROUPS:
                    act.wait_ge(hp_made, NG * (a + (g > 4)) + b + 1)
                    act.activation(hp_exp[:, t0:t0 + n, :], hp[:, t0:t0 + n, :], ACT.Exp).then_inc(hp_exp_made, 1)

            def mixture(f):
                E, kind = MOES[f]
                base = EXPERTS_BEFORE[f]
                exps = [0, 1, 3][f]
                def high_in(e, b, k, first=False):
                    act.wait_ge(experts_in[b], LOADED_BEFORE[f] + 16 * LOADS[f] * (k + 1))
                    if not first or f > 0:
                        act.wait_ge(unit_made, UNITS * (base + e - 1))
                    act.activation(w_hi[b][:, 0:SPLIT[f]], w_exp[b][:, 0:SPLIT[f]], ACT.Copy).then_inc(in_w_high, 1)

                def units(e, b, k, first=False, last=False):
                    if kind != "silu" and (not first or f > 0):
                        act.wait_ge(expert_used, base + e - 1)
                    for u in range(UNITS):
                        half, c = divmod(u, NCH)
                        c0, w = CHUNKS[c]
                        act.wait_ge(unit_made, UNITS * (base + e) + u + 1)
                        if kind == "silu":
                            s = u % 2
                            if not first or b or u >= 2:
                                act.wait_ge(hid_made, UNITS * (base + e) + u - 1)
                            act.activation(silu[s][:, 0:w], ps[:, 3 + 2 * s, 0:w], ACT.Silu).then_inc(silu_made, 1)
                        else:
                            s = (UNITS * b + u) % 4
                            bias = w_exp[b][:, BIAS_AT + half:BIAS_AT + half + 1]
                            act.activation(hid[b][:, half, c0:c0 + w], ps[:, 3 + s, 0:w], ACT.Relu,
                                           bias=bias).then_inc(hid_made, 1)
                        if u == NCH - 1 and first and b and f < 2:
                            act.wait_ge(disp_turned, f + 1)
                            rows = ps[0:E, 0:NCH, :].rearrange("p b n -> p (b n)")[:, 0:NP]
                            act.activation(dispT[0:E, :], rows, ACT.Copy).then_inc(dispT_made, 1)
                        if u == NCH - 1 and not last:
                            high_in(e + 1, 1 - b, k + b, first and b == 0)

                def exponentials():
                    n = [0, 1, 3][f]
                    if kind == "relu2":
                        act.wait_ge(top_diff_made, n + 1)
                        act.activation(route_exp[:, :, 0:E], logits[:, :, 0:E], ACT.Exp)
                        act.activation(top_w[:, :, 1], top_w[:, :, 0], ACT.Exp).then_inc(top_exp_made, 1)
                        n += 1
                    act.wait_ge(top_diff_made, n + 1)
                    act.activation(top_w[:, :, 1], top_w[:, :, 0], ACT.Exp).then_inc(top_exp_made, 1)

                high_in(0, 0, 0, first=True)
                if kind == "relu2":
                    act.wait_ge(router_rows, 1)
                    rows = ps[0:64, ROW_BANKS:ROW_BANKS + NCH, :].rearrange("p b n -> p (b n)")[:, 0:NP]
                    act.activation(router_h[:], rows, ACT.Relu, bias=router_b1[:]).then_inc(router_h_made, 1)
                units(0, 0, 0, first=True)
                exponentials()
                units(1, 1, 0, first=True)
                with act.Fori(1, E // 2 - 1) as k:
                    units(2 * k, 0, k)
                    units(2 * k + 1, 1, k)
                units(E - 2, 0, E // 2 - 1)
                units(E - 1, 1, E // 2 - 1, last=True)

            for dst, src in gat_loads:
                act.dma_start(dst, src).then_inc(gat_in, 16)
            normed_rows("G0")
            for t in range(NT):
                act.wait_ge(adj_used, t + 1)
                if t:
                    act.wait_ge(degree_made, t)
                mask = mask_nat[t % AHEAD] if t < NT - 1 else mask_last
                act.activation(count_junk, mask[:, 0:N], ACT.Copy, accum_out=degree[:, t:t + 1]).then_inc(degree_made, 1)
            attention(0)
            normed_rows("F0")
            mixture(0)
            normed_rows("G1n")
            copy_rows("G1a")
            attention(1)
            copy_rows("G1b")
            attention(2)
            copy_rows("G1c")
            attention(3)
            normed_rows("F1")
            mixture(1)
            normed_rows("G2")
            attention(4)
            for c in range(NCH):
                normalise("in G2", hp, hp_exp, c)
            normed_rows("F2")
            normed_rows("G3")
            attention(5)
            normed_rows("F3")
            mixture(2)

        @block.vector
        def _(dve):
            chain = 0

            def link(ins):
                nonlocal chain
                chain += 1
                ins.then_inc(dve_done, 1)
                dve.wait_ge(dve_done, chain)

            def each(ap, n):
                return ap.unsqueeze(2).to_broadcast([P, ap.shape[1], n])

            def along_tiles(ap):
                return ap.unsqueeze(1).to_broadcast([P, NT, ap.shape[1]])

            def statistics(src, c):
                c0, w = CHUNKS[c]
                tiles = range(c0 // P, (c0 + w) // P)
                part = slice(tiles[0], tiles[-1] + 1)
                for t in tiles:
                    ins = dve.bn_stats(stats[:, t, :], src[:, t, :])
                link(ins)
                for t in tiles:
                    ins = dve.bn_aggr(moments[:, t, :], stats[:, t, :])
                link(ins)
                dve.tensor_scalar(var_eps[:, part], moments[:, part, 1], LN_EPS, None, ALU.add)
                dve.tensor_scalar(neg_mean[:, part], moments[:, part, 0], -1.0, None, ALU.mult).then_inc(var_made, 1)

            def apply(name, src, dst, c):
                dve.wait_ge(rstd_made, NCH * NORMS[name] + c + 1)
                for t in halves(c)[0]:
                    ins = dve.tensor_scalar(dst[:, t, :], src[:, t, :], moments[:, t, 0:1], rstd[:, t:t + 1],
                                            ALU.subtract, ALU.mult)
                ins.then_inc(xn_dve, 1)

            def normalise(name, before=lambda c: None, src=x, dst=xn):
                before(0)
                statistics(src, 0)
                for c in range(1, NCH):
                    before(c)
                    statistics(src, c)
                    apply(name, src, dst, c - 1)
                apply(name, src, dst, NCH - 1)

            def attention(g, then=None):
                name, alpha = GATS[g]
                a = SCORED.index(g) if alpha is not None else None
                PROBS = NCH + NT - 1
                dve.wait_ge(inT_made, NCH * (INPUTS[name] + 1))
                dve.reduce_sum(inT[:, N:N + 1], sum_parts[:], AX_X).then_inc(sum_made, 1)
                if alpha is None:
                    for i, tiles in enumerate((slice(0, SLOTS), slice(SLOTS, NT))):
                        dve.wait_ge(wh_copied, NG * g + (1 if i == 0 else NG))
                        rest = wh[:, tiles, :]
                        for q in range(3):
                            dve.tensor_copy(wh_part[q][:, tiles, :], rest).then_inc(wh_split, 1)
                            if q < 2:
                                dve.wait_ge(wh_split, 5 * i + 2 * q + 1)
                                dve.tensor_tensor(wh_rest[:, tiles, :], rest, wh_part[q][:, tiles, :],
                                                  ALU.subtract).then_inc(wh_split, 1)
                                dve.wait_ge(wh_split, 5 * i + 2 * q + 2)
                                rest = wh_rest[:, tiles, :]
                else:
                    dve.wait_ge(f2_made, a + 1)
                    link(dve.tensor_reduce(f2_top[:], ps[:, MISC, 0:NT - 1], AX_X, ALU.max))
                    dve.tensor_tensor(f2_top[0:LAST, :], f2_top[0:LAST, :], ps[0:LAST, MISC, NT - 1:NT],
                                      ALU.max).then_inc(f2_top_made, 1)
                    dve.wait_ge(f2_top_turned, a + 1)
                    dve.tensor_reduce(f2_top_all[:], ps[0:1, MISC, NT + 1:NT + 1 + P], AX_X, ALU.max).then_inc(f2_top_all_made, 1)
                    dve.wait_ge(f2_max_spread, a + 1)
                    link(dve.tensor_copy(f2_max[:], ps[:, MISC, NT:NT + 1]))
                    link(dve.scalar_tensor_tensor(f2_shift[:], ps[:, MISC, 0:NT], f2_max[:], real[:], ALU.subtract, ALU.mult))
                    dve.tensor_scalar(f2_alpha[:], f2_shift[:], alpha, None, ALU.mult).then_inc(f2_shifted, 1)
                    for c, (c0, w) in enumerate(CHUNKS):
                        dve.wait_ge(f1_made, NCH * a + c + 1)
                        dve.tensor_scalar(f1_pos[:, c0:c0 + w], row_bank(c), f2_max[:], 0.0, ALU.add, ALU.max).then_inc(f1_read, 1)
                    dve.wait_ge(f2_exp_made, a + 1)
                    for c, (c0, w) in enumerate(CHUNKS):
                        dve.wait_ge(low_made, PROBS * a + c + 1)
                        dve.scalar_tensor_tensor(prob[0][:, c0:c0 + w], low[0][:, c0:c0 + w], f2_exp[:, 0:1],
                                                 maskT[:, 0, c0:c0 + w], ALU.max, ALU.mult).then_inc(prob_made, 1)

                    def weights(j, b, first=False):
                        if not first:
                            dve.wait_ge(prob_used, (NT - 1) * a + j - 1)
                        mask = maskT[:, bass.ds(j, 1), :].rearrange("p o n -> p (o n)")
                        dve.wait_ge(low_made, PROBS * a + NCH + j)
                        dve.scalar_tensor_tensor(prob[b][:], low[b][:], f2_exp[:, bass.ds(j, 1)], mask,
                                                 ALU.max, ALU.mult).then_inc(prob_made, 1)

                    weights(1, 1, first=True)
                    with dve.Fori(1, (NT - 1) // 2) as k:
                        weights(2 * k, 0)
                        weights(2 * k + 1, 1)
                    weights(NT - 1, 0)
                for b, t0, n in GROUPS:
                    dve.wait_ge(att_made, NG * g + b + 1)
                    acc = tiles_in(b, n, AW)
                    link(dve.reciprocal(inv_sum[:, t0:t0 + n], acc[:, :, D]))
                    dve.tensor_tensor(hp[:, t0:t0 + n, :], acc[:, :, 0:D], each(inv_sum[:, t0:t0 + n], D),
                                      ALU.mult).then_inc(hp_made, 1)
                if alpha is None:
                    dve.wait_ge(hp_made, NG * (g + 1))
                    return
                if then is None:
                    for b, t0, n in GROUPS:
                        dve.wait_ge(hp_exp_made, NG * a + b + 1)
                        e = hp_exp[:, t0:t0 + n, :]
                        h = hp[:, t0:t0 + n, :]
                        link(dve.tensor_scalar(e, e, 1.0, -1.0, ALU.min, ALU.add))
                        dve.tensor_tensor(h, h, e, ALU.max).then_inc(elu_made, 1)
                    return
                dve.wait_ge(x_shifted, {0: 1, 3: 2, 5: 4}[g])
                added = 0

                def add_elu(c):
                    nonlocal added
                    while added * SLOTS < sum(CHUNKS[c]) // P:
                        b, t0, n = GROUPS[added]
                        xs = x[:, t0:t0 + n, :]
                        dve.wait_ge(hp_exp_made, NG * a + b + 1)
                        link(dve.scalar_tensor_tensor(xs, hp[:, t0:t0 + n, :], 0.0, xs, ALU.max, ALU.add))
                        link(dve.scalar_tensor_tensor(xs, hp_exp[:, t0:t0 + n, :], 1.0, xs, ALU.min, ALU.add))
                        added += 1

                normalise(then, add_elu)

            def mixture(f, then=None):
                E, kind = MOES[f]
                base = EXPERTS_BEFORE[f]
                exps = [0, 1, 3][f]
                lg = logits[:, :, 0:E]
                wide = max(E, 8)
                for c, (c0, w) in enumerate(CHUNKS):
                    dve.wait_ge(inT_made, NCH * INPUTS[("F0", "F1", "F3")[f]] + c + 1)
                    dve.tensor_copy(in_hi[:, c0:c0 + w], inT[:, c0:c0 + w]).then_inc(in_hi_made, 1)
                    dve.wait_ge(in_hi_made, NCH * f + c + 1)
                    dve.tensor_tensor(in_lo[:, c0:c0 + w], inT[:, c0:c0 + w], in_hi[:, c0:c0 + w].bitcast(F32),
                                      ALU.subtract).then_inc(in_lo_made, 1)
                def units(e, b):
                    for u in range(UNITS if kind == "silu" else 0):
                        half, c = divmod(u, NCH)
                        c0, w = CHUNKS[c]
                        dve.wait_ge(silu_made, UNITS * e + u + 1)
                        dve.tensor_tensor(hid[b][:, half, c0:c0 + w], silu[u % 2][:, 0:w],
                                          ps[:, 4 + 2 * (u % 2), 0:w], ALU.mult).then_inc(hid_made, 1)

                def combine(e, first=False, chunks=range(NCH), last=False):
                    if not first:
                        dve.wait_ge(y_used, base - f + e)
                    for c in chunks:
                        c0, w = CHUNKS[c]
                        if c < NCH - 1:
                            dve.wait_ge(y_made, (NCH - 1) * (base + e) + c + 1)
                        else:
                            dve.wait_ge(expert_used, base + e + 1)
                        for t in range(c0 // P, (c0 + w) // P):
                            ins = dve.scalar_tensor_tensor(x[:, t, :], tile_out(t), disp[:, t, bass.ds(e, 1)], x[:, t, :],
                                                           ALU.mult, ALU.add)
                        if last and f == 2:
                            ins.then_inc(x_done, 1)
                        elif last:
                            link(ins)
                    if not last:
                        ins.then_inc(y_used, 1)

                units(0, 0)
                dve.wait_ge(logits_made, f + 1)
                if wide > E:
                    dve.memset(logits[:, :, E:wide], -1e30)
                link(dve.tensor_tensor(lg, tiles_in(MISC, NT, E), along_tiles(gate_b[f][:]), ALU.add))
                if f == 0:
                    link(dve.tensor_tensor(lg, lg, along_tiles(gate_b_more[:]), ALU.add))
                for t in range(NT):
                    ins = dve.max(top[:, t, :], logits[:, t, 0:wide])
                link(ins)
                for t in range(NT):
                    ins = dve.max_index(top_at[:, t, :], top[:, t, :], logits[:, t, 0:wide])
                link(ins)
                link(dve.tensor_copy(top_at_f[:, :, 0:2], top_at[:, :, 0:2]))
                if kind == "relu2":
                    link(dve.tensor_tensor(lg, lg, each(top[:, :, 0], E), ALU.subtract))
                    dve.tensor_tensor(top_w[:, :, 0], top[:, :, 1], top[:, :, 0], ALU.subtract).then_inc(top_diff_made, 1)
                    exps += 1
                    dve.wait_ge(top_exp_made, exps)
                    link(dve.reduce_sum(route_sum[:], route_exp[:, :, 0:E], AX_X))
                    link(dve.reciprocal(top_w[:, :, 2], route_sum[:]))
                    link(dve.tensor_scalar(top_w[:, :, 1], top_w[:, :, 1], -1.0, None, ALU.add))
                    dve.tensor_tensor(top_w[:, :, 0], top_w[:, :, 1], top_w[:, :, 2], ALU.mult).then_inc(top_diff_made, 1)
                else:
                    dve.tensor_tensor(top_w[:, :, 0], top[:, :, 1], top[:, :, 0], ALU.subtract).then_inc(top_diff_made, 1)
                dve.wait_ge(top_exp_made, exps + 1)
                link(dve.tensor_scalar(top_w[:, :, 3], top_w[:, :, 1], 1.0, None, ALU.add))
                link(dve.reciprocal(top_w[:, :, 2], top_w[:, :, 3]))
                link(dve.tensor_tensor(top_w[:, :, 3], top_w[:, :, 1], top_w[:, :, 2], ALU.mult))
                places = along_tiles(iota_e[:, 0:E])
                for q, dst in enumerate((disp, disp_2)):
                    link(dve.tensor_tensor(dst[:, :, 0:E], places, each(top_at_f[:, :, q], E), ALU.is_equal))
                    link(dve.tensor_tensor(dst[:, :, 0:E], dst[:, :, 0:E], each(top_w[:, :, 2 + q], E), ALU.mult))
                dve.tensor_tensor(disp[:, :, 0:E], disp[:, :, 0:E], disp_2[:, :, 0:E], ALU.add).then_inc(disp_made, 1)
                dve.wait_ge(disp_made, f + 1)

                if f < 2:
                    dve.wait_ge(bias_made, f + 1)
                    dve.tensor_tensor(x[:], x[:], ps[:, 0:NCH, :].rearrange("p b n -> p (b n)")[:, 0:NP]
                                      .rearrange("p (t d) -> p t d", d=D), ALU.add).then_inc(bias_added, 1)
                    dve.wait_ge(bias_added, f + 1)
                if f == 0:
                    for g in SCORED[1:]:
                        ins = attention_weights(g)
                    ins.then_inc(weights_made, 1)

                def step(e, b, first=False):
                    units(e, b)
                    combine(e - 1, first)

                step(1, 1, first=True)
                with dve.Fori(1, E // 2) as k:
                    step(2 * k, 0)
                    step(2 * k + 1, 1)
                if then is None:
                    combine(E - 1, last=True)
                else:
                    normalise(then, lambda c: combine(E - 1, chunks=[c], last=True))

            def attention_weights(g):
                for h in range(2):
                    link(dve.tensor_tensor_reduce(dot_junk[:], w_gat[:, g, :], a_row[g][:, h * D:(h + 1) * D], 1.0, 0.0,
                                                  ALU.mult, ALU.add, wa[:, g, h:h + 1]))
                return dve.tensor_scalar(wa1_rep[g][:], ones[:], wa[:, g, 0:1], None, ALU.mult)

            dve.memset(x[:, NT - 1, :], 0.0).then_inc(pad_cleared, 1)
            dve.wait_ge(x_in, X_LOADS)
            normalise("G0")
            dve.wait_ge(gat_in, GAT_LOADED)
            dve.wait_ge(consts_made, 1)
            dve.tensor_copy(wh[:, :, D], count[:])
            attention_weights(0).then_inc(weights_made, 1)

            def make(t):
                dve.wait_ge(adj_in[t % AHEAD], 16 * (t // AHEAD + 1))
                rows = P if t < NT - 1 else LAST
                mask = mask_nat[t % AHEAD] if t < NT - 1 else mask_last
                if t >= AHEAD:
                    dve.wait_ge(mask_turned, t - AHEAD + 1)
                dve.tensor_scalar(mask[0:rows, 0:N], adj_i[t % AHEAD][0:rows, :], 0, None, ALU.is_gt).then_inc(adj_used, 1)

            def finish(t):
                dve.wait_ge(degree_made, t + 1)
                mask = mask_nat[t % AHEAD] if t < NT - 1 else mask_last
                dve.tensor_scalar(mask[:, N:N + 1], degree[:, t:t + 1], 0.0, None, ALU.is_equal).then_inc(mask_made, 1)

            def copy_out(t):
                dve.wait_ge(mask_turned, t + 1)
                half = 2 * (t % 2)
                src = ps[:, half:half + 2, :].rearrange("p b n -> p (b n)").bitcast(BF16)[:, 0:NP]
                dve.tensor_copy(maskT[:, :, cols(t)], src.rearrange("p (j n) -> p j n", n=P)).then_inc(mask_copied, 1)

            dve.wait_ge(mask_cleared, 1)
            for t in range(AHEAD - 1):
                make(t)
            for t in range(NT):
                finish(t)
                if t:
                    copy_out(t - 1)
                if t + AHEAD - 1 < NT:
                    make(t + AHEAD - 1)
            copy_out(NT - 1)

            attention(0, "F0")
            mixture(0, "G1n")
            attention(1)
            attention(2)
            attention(3, "F1")
            mixture(1, "G2")
            attention(4)

            def finish_l2(c):
                c0, w = CHUNKS[c]
                part = slice(c0 // P, (c0 + w) // P)
                dve.wait_ge(xn_act, NCH * NORMS["in G2"] + c + 1)
                dve.wait_ge(xn_dve, NCH * NORMS["in G2"] + c + 1)
                n = part.stop - part.start
                e = hp_exp[:, part, :]
                link(dve.tensor_tensor(e, e, gamma[:].unsqueeze(1).to_broadcast([P, n, D]), ALU.mult))
                link(dve.tensor_tensor(x[:, part, :], x[:, part, :], e, ALU.add))

            normalise("in G2", src=hp, dst=hp_exp)
            dve.wait_ge(x_shifted, 3)
            normalise("F2", finish_l2)

            def add_linear(c):
                c0, w = CHUNKS[c]
                dve.wait_ge(lin_made, c + 1)
                part = slice(c0 // P, (c0 + w) // P)
                out = ps[:, c, 0:w].rearrange("p (t d) -> p t d", d=D)
                link(dve.tensor_tensor(x[:, part, :], x[:, part, :], out, ALU.add))

            normalise("G3", add_linear)
            attention(5, "F3")
            mixture(2)


OUTPUT = "out"


def kernel(**inputs):
    import numpy as np
    import concourse.bacc as bacc
    from concourse.bass_utils import run_bass_kernel_spmd

    nc = bacc.Bacc("TRN2", target_bir_lowering=False, num_devices=1)
    arrays, io = {}, {}
    for name, value in inputs.items():
        if name == "L1_ffn_expert_b2":
            continue
        if name == "L2_gnn_a":
            continue
        a = np.asarray(value)
        if name == "L0_ffn_b1":
            a = a.reshape(a.shape[0], 2, P).transpose(0, 2, 1)
        elif name == "L1_ffn_expert_b1":
            name, a = "L1_ffn_expert_b12", np.stack([a, np.asarray(inputs["L1_ffn_expert_b2"])], axis=-1)
        elif name == "L2_ffn_weight":
            a = a.T
        a = np.ascontiguousarray(a)
        arrays[f"in_{name}"] = a
        io[name] = nc.dram_tensor(f"in_{name}", a.shape, mybir.dt.from_np(a.dtype), kind="ExternalInput").ap()
    io["out"] = nc.dram_tensor("out", inputs["x"].shape, F32, kind="ExternalOutput").ap()
    build(nc, io)
    result = run_bass_kernel_spmd(nc, [arrays], core_ids=[0])
    return result.results[0]["out"]
```

```python
from contextlib import ExitStack

import concourse.bass as bass
from concourse import mybir

F32 = mybir.dt.float32
F32R = mybir.dt.float32r
BF16 = mybir.dt.bfloat16
I32 = mybir.dt.int32
U32 = mybir.dt.uint32
ALU = mybir.AluOpType
ACT = mybir.ActivationFunctionType
AX_X = mybir.AxisListType.X

P = 128
D = 128
LN_EPS = 1e-5
BANK = 512
AW = D + 1
SLOTS = 3

GATS = [("G0", 0.2), ("G1a", 0.01), ("G1b", 0.01), ("G1c", 0.01), ("G2", None), ("G3", 0.2)]
SCORED = [g for g, (_, alpha) in enumerate(GATS) if alpha is not None]
MOES = [(8, "relu"), (6, "relu2"), (16, "silu")]
BIAS_AT = 768
OUT_AT, OUT_END = [256, 256, 512], [512, 384, 768]
SPLIT = [256, 128, 512]
ADJ_AHEAD = 6
AHEAD = 4
HEAD_KEEP = 6
KEEP_A, KEEP_B = 12, 12
UNITS = 6


def build(nc, io):
    N = io["x"].shape[0]
    NT = -(-N // P)
    NP = NT * P
    LAST = N - (NT - 1) * P
    CHUNKS = [(c, min(BANK, NP - c)) for c in range(0, NP, BANK)]
    NCH = len(CHUNKS)
    NODE_CHUNKS = [(c, min(w, N - c)) for c, w in CHUNKS]
    assert N % 2 == 0
    GROUPS = [(b, b * SLOTS, min(SLOTS, NT - b * SLOTS)) for b in range(-(-NT // SLOTS))]
    NG = len(GROUPS)
    TPB = BANK // P
    assert NT % 2 == 1 and LAST < P

    EXPERTS_BEFORE = [sum(e for e, _ in MOES[:f]) for f in range(len(MOES))]

    with ExitStack() as ctx:
        def sb(name, shape, dt=F32):
            return ctx.enter_context(nc.sbuf_tensor(name, shape, dt))

        def sem(name):
            return ctx.enter_context(nc.semaphore(name))

        x = sb("x", [P, NT, D])
        xn = sb("xn", [P, NT, D])
        inT = sb("inT", [P, NP])
        maskT = sb("maskT", [P, NT, NP], BF16)
        degree = sb("degree", [P, NT])
        ident = sb("ident", [P, P])
        ident_h = sb("ident_h", [P, P], BF16)
        ones = sb("ones", [P, P])
        real = sb("real", [P, NT])
        count = sb("count", [P, NT])
        minus_half = sb("minus_half", [P, NT])
        iota_e = sb("iota_e", [P, 16])

        stats = sb("stats", [P, NT, 6])
        moments = sb("moments", [P, NT, 2])
        var_eps = sb("var_eps", [P, NT])
        rstd = sb("rstd", [P, NT])
        neg_mean = sb("neg_mean", [P, NT])
        shift = sb("shift", [P, NT])

        w_gat = sb("w_gat", [P, len(GATS), AW])
        a_row = [sb(f"a_row{g}", [P, 2 * D]) for g in range(len(GATS))]
        wa1 = sb("wa1", [P, len(GATS)])
        wa1_rep = [sb(f"wa1_rep{g}", [P, P]) for g in range(len(GATS))]
        dot_junk = sb("dot_junk", [P, D])
        w0_T = sb("w0_T", [P, D])
        w1_ext = sb("w1_ext", [P, AW + 1])
        wh = sb("wh", [P, NT, AW + 1])
        sum_parts = sb("sum_parts", [P, NCH])
        f2_top = sb("f2_top", [P, 1])
        f2_top_all = sb("f2_top_all", [1, 1])
        f2_shift = sb("f2_shift", [P, NT])
        f2_alpha = sb("f2_alpha", [P, NT])
        f2_exp = sb("f2_exp", [P, NT])
        f1_pos = sb("f1_pos", [P, NP])
        low = [sb(f"low{b}", [P, NP]) for b in range(2)]
        prob = [sb(f"prob{b}", [P, NP]) for b in range(2)]
        count_junk = f1_pos[:, 0:NP // 2].bitcast(BF16)[:, 0:N]
        inv_sum = sb("inv_sum", [P, NT])
        hp = sb("hp", [P, NT, D])
        hp_exp = sb("hp_exp", [P, NT, D])
        adj_i = [buf[:, 0:N].bitcast(I32) for buf in low + prob] + [
            buf[:, :, :].rearrange("p t d -> p (t d)")[:, 0:N].bitcast(I32) for buf in (hp, hp_exp)]

        gate_w = [sb("gate_w0", [P, 8]), sb("gate_w1", [64, 6]), sb("gate_w2", [P, 16])]
        gate_b = [sb(f"gate_b{f}", [P, e]) for f, (e, _) in enumerate(MOES)]
        gate_b_more = sb("gate_b_more", [P, 8])
        router_w1 = sb("router_w1", [P, 64])
        router_b1 = sb("router_b1", [64, 1])
        router_h = sb("router_h", [64, NP])
        logits = sb("logits", [P, NT, 16])
        route_exp = sb("route_exp", [P, NT, 16])
        route_sum = sb("route_sum", [P, NT])
        top = sb("top", [P, NT, 8])
        top_at = sb("top_at", [P, NT, 8], U32)
        top_at_f = sb("top_at_f", [P, NT, 8])
        top_w = sb("top_w", [P, NT, 4])
        disp = sb("disp", [P, NT, 16])
        disp_2 = sb("disp_2", [P, NT, 16])
        dispT = sb("dispT", [8, NP])
        bias_out = [sb("bias_out0", [8, D]), sb("bias_out1", [6, D])]
        w_exp = [sb(f"w_exp{b}", [P, BIAS_AT + 2]) for b in range(2)]
        w_hi = [sb(f"w_hi{b}", [P, max(SPLIT)], F32R) for b in range(2)]
        w_lo = [sb(f"w_lo{b}", [P, max(SPLIT)], F32R) for b in range(2)]
        in_hi = sb("in_hi", [P, NP], F32R)
        in_lo = sb("in_lo", [P, NP], F32R)
        hid = [sb(f"hid{b}", [P, 2, NP]) for b in range(2)]
        mask_nat = [hid[q // 2][:, q % 2, :].bitcast(BF16)[:, 0:NP] for q in range(AHEAD)]
        mask_last = sb("mask_last", [P, NP], BF16)
        wh_part = [hid[0][:, h, :].bitcast(BF16)[:, 0:NT * AW].rearrange("p (t w) -> p t w", w=AW) for h in range(2)] + [
            hid[1][:, 0, :].bitcast(BF16)[:, 0:NT * AW].rearrange("p (t w) -> p t w", w=AW)]
        wh_rest = sb("wh_rest", [P, NT, AW])
        silu = [f1_pos[:, b * BANK:(b + 1) * BANK] for b in range(2)]
        table_scratch = sb("table_scratch", [P, 1])
        lin_wT = sb("lin_wT", [P, D])
        lin_b = sb("lin_b", [1, D])
        gamma = sb("gamma", [P, D])
        beta = sb("beta", [P, D])

        ps = ctx.enter_context(nc.psum_tensor("ps", [P, 8, BANK], F32))
        TILE_BANKS, ROW_BANKS, MISC = 0, 4, 7

        def tiles_in(bank, n, width):
            return ps[:, bank, 0:n * width].rearrange("p (s w) -> p s w", w=width)

        f2_max = ps[:, MISC, 0:1]

        def row_bank(c):
            return ps[:, ROW_BANKS + c, 0:CHUNKS[c][1]]

        def tile_out(t, rows=P):
            return ps[0:rows, t // TPB, (t % TPB) * P:(t % TPB + 1) * P]

        def nodes_of(t):
            return P if t < NT - 1 else LAST

        def cols(t):
            return slice(t * P, (t + 1) * P)

        x_in = sem("x_in")
        adj_in = [sem(f"adj_in{b}") for b in range(ADJ_AHEAD)]
        gat0_in = sem("gat0_in")
        gat_in = sem("gat_in")
        params_in = sem("params_in")
        experts_in = [sem(f"experts_in{b}") for b in range(2)]
        experts_out_in = [sem(f"experts_out_in{b}") for b in range(2)]
        out_stored = sem("out_stored")
        pool_made = sem("pool_made")
        consts_made = sem("consts_made")
        dve_done = sem("dve_done")
        act_done = sem("act_done")
        pad_cleared = sem("pad_cleared")
        mask_cleared = sem("mask_cleared")
        adj_used = sem("adj_used")
        mask_made = sem("mask_made")
        degree_made = sem("degree_made")
        mask_turned = sem("mask_turned")
        mask_copied = sem("mask_copied")
        weights_made = sem("weights_made")
        w01_made = sem("w01_made")
        var_made = sem("var_made")
        rstd_made = sem("rstd_made")
        xn_dve = sem("xn_dve")
        xn_act = sem("xn_act")
        x_shifted = sem("x_shifted")
        relu_made = sem("relu_made")
        relu_added = sem("relu_added")
        elu_made = sem("elu_made")
        x_done = sem("x_done")
        rows_made = sem("rows_made")
        inT_made = sem("inT_made")
        sum_made = sem("sum_made")
        f2_top_made = sem("f2_top_made")
        f2_top_turned = sem("f2_top_turned")
        f2_top_all_made = sem("f2_top_all_made")
        f2_max_spread = sem("f2_max_spread")
        f1_made = sem("f1_made")
        f1_read = sem("f1_read")
        wh_made = sem("wh_made")
        wh_copied = sem("wh_copied")
        f2_shifted = sem("f2_shifted")
        f2_exp_made = sem("f2_exp_made")
        low_made = sem("low_made")
        prob_made = sem("prob_made")
        prob_used = sem("prob_used")
        att_made = sem("att_made")
        hp_made = sem("hp_made")
        hp_exp_made = sem("hp_exp_made")
        router_rows = sem("router_rows")
        router_h_made = sem("router_h_made")
        logits_made = sem("logits_made")
        logits_read = sem("logits_read")
        top_diff_made = sem("top_diff_made")
        top_exp_made = sem("top_exp_made")
        disp_made = sem("disp_made")
        disp_turned = sem("disp_turned")
        dispT_made = sem("dispT_made")
        bias_made = sem("bias_made")
        bias_added = sem("bias_added")
        unit_made = sem("unit_made")
        gate_made = sem("gate_made")
        silu_made = sem("silu_made")
        hid_made = sem("hid_made")
        in_w_split = sem("in_w_split")
        in_w_high = sem("in_w_high")
        in_hi_made = sem("in_hi_made")
        in_lo_made = sem("in_lo_made")
        wh_split = sem("wh_split")
        y_made = sem("y_made")
        y_used = sem("y_used")
        expert_used = sem("expert_used")
        lin_made = sem("lin_made")

        INPUTS = {name: i for i, name in enumerate(
            ["G0", "F0", "G1a", "G1b", "G1c", "F1", "G2", "F2", "G3", "F3"])}
        NORMS = {name: i for i, name in enumerate(["G0", "F0", "G1a", "F1", "G2", "in G2", "F2", "G3", "F3"])}
        SUMMED = ("G0", "G1a", "G1b", "G1c", "G2", "G3")

        GAT_PARAMS = [("L0_gnn_W", "L0_gnn_a"), ("L1_gnn_W1", "L1_gnn_a1"), ("L1_gnn_W2", "L1_gnn_a2"),
                      ("L1_gnn_W3", "L1_gnn_a3"), ("L2_gnn_W", None), ("L3_gnn_W", "L3_gnn_a")]

        def row(name, lo, hi):
            ap = io[name]
            flat = ap.rearrange("a b -> (a b)") if len(ap.shape) == 2 else ap
            return flat[lo:hi].rearrange("(o n) -> o n", o=1).to_broadcast([P, hi - lo])

        gat_loads, param_loads = [], []
        for g, (w, a) in enumerate(GAT_PARAMS):
            gat_loads.append((w_gat[:, g, 0:D], io[w]))
            if a:
                gat_loads.append((a_row[g][:], row(a, 0, 2 * D)))
        param_loads += [
            (w0_T[:], io["L1_gnn_W0"]),
            (gate_w[0][:], io["L0_ffn_Wg"]), (gate_w[1][:], io["L1_ffn_router_w2"]),
            (gate_w[2][:], io["L3_ffn_gate_w"]),
            (gate_b[0][:], row("L0_ffn_bg", 0, 8)), (gate_b_more[:], row("L0_ffn_bias", 0, 8)),
            (gate_b[1][:], row("L1_ffn_router_b2", 0, 6)), (gate_b[2][:], row("L3_ffn_gate_b", 0, 16)),
            (router_w1[:], io["L1_ffn_router_w1"]),
            (router_b1[:], io["L1_ffn_router_b1"].rearrange("(p o) -> p o", o=1)),
            (bias_out[0][:], io["L0_ffn_b2"]), (bias_out[1][:], io["L1_ffn_expert_b3"]),
            (lin_wT[:], io["L2_ffn_weight"]), (lin_b[:], io["L2_ffn_bias"].rearrange("(o n) -> o n", o=1)),
            (gamma[:], row("L2_gnn_gamma", 0, D)), (beta[:], row("L2_gnn_beta", 0, D)),
        ]
        GAT_LOADED, PARAMS = 16 * (len(gat_loads) - 2), 16 * len(param_loads)

        ADDED_ELU = [0, 3, 5]

        def halves(c):
            t0, n = CHUNKS[c][0] // P, CHUNKS[c][1] // P
            mine = 1 if c < NCH - 1 else (n + 1) // 2
            return range(t0, t0 + mine), range(t0 + mine, t0 + n)
        X_LOADS = 32

        def expert_loads(f, e, b):
            def one(name):
                return io[name][bass.ds(e, 1)].rearrange("e p n -> (e p) n")
            biases = w_exp[b][:, BIAS_AT:BIAS_AT + 2]
            if f == 0:
                return [(w_exp[b][:, 0:256], one("L0_ffn_W1")), (biases, one("L0_ffn_b1"))]
            if f == 1:
                return [(w_exp[b][:, i * P:(i + 1) * P], one(f"L1_ffn_expert_w{i + 1}")) for i in range(2)] + [
                    (biases, one("L1_ffn_expert_b12"))]
            return [(w_exp[b][:, 0:256], one("L3_ffn_w1")), (w_exp[b][:, 256:512], one("L3_ffn_w2"))]

        def output_load(f, e, b):
            src = io[["L0_ffn_W2", "L1_ffn_expert_w3", "L3_ffn_w3"][f]][bass.ds(e, 1)]
            n = OUT_END[f] - OUT_AT[f]
            return (w_exp[b][:, OUT_AT[f]:OUT_END[f]].rearrange("p (c n) -> p c n", n=D),
                    src.rearrange("e (c p) n -> (e p) c n", c=n // D))

        LOADS = [2, 3, 2]
        LOADED_BEFORE = [sum(16 * LOADS[q] * (MOES[q][0] // 2) for q in range(f)) for f in range(len(MOES))]
        OUT_LOADED_BEFORE = [16 * EXPERTS_BEFORE[f] // 2 for f in range(len(MOES))]

        block = ctx.enter_context(nc.Block())

        @block.sync
        def _(sp):
            sp.dma_start(x[:, 0:NT - 1, :], io["x"][0:(NT - 1) * P, :].rearrange("(t p) d -> p t d", p=P)).then_inc(x_in, 16)
            sp.wait_ge(pad_cleared, 1)
            sp.dma_start(x[0:LAST, NT - 1, :], io["x"][(NT - 1) * P:N, :]).then_inc(x_in, 16)
            for t in range(NT):
                rows = P if t < NT - 1 else LAST
                if t >= ADJ_AHEAD:
                    sp.wait_ge(adj_used, t - ADJ_AHEAD + 1)
                b = t % ADJ_AHEAD
                sp.dma_start(adj_i[b][0:rows, :], io["adj"][t * P:t * P + rows, :]).then_inc(adj_in[b], 16)
            for f, (E, _) in enumerate(MOES):
                def load(e, b, first=False):
                    if not first or f > 0:
                        sp.wait_ge(hid_made, UNITS * (EXPERTS_BEFORE[f] + e - 1))
                    if first and f > 0:
                        sp.wait_ge(expert_used, EXPERTS_BEFORE[f] + e - 1)
                    for dst, src in expert_loads(f, e, b):
                        sp.dma_start(dst, src).then_inc(experts_in[b], 16)
                    if not first:
                        sp.wait_ge(expert_used, EXPERTS_BEFORE[f] + e - 1)
                    sp.dma_start(*output_load(f, e, b)).then_inc(experts_out_in[b], 16)
                for b in range(2):
                    load(b, b, first=True)
                with sp.Fori(1, E // 2) as k:
                    for b in range(2):
                        load(2 * k + b, b)
            for c, (c0, w) in enumerate(CHUNKS):
                sp.wait_ge(x_done, c + 1)
                full = min(w, (NT - 1) * P - c0)
                sp.dma_start(io["out"][c0:c0 + full, :].rearrange("(t p) d -> p t d", p=P),
                             x[:, c0 // P:(c0 + full) // P, :]).then_inc(out_stored, 16)
            sp.dma_start(io["out"][(NT - 1) * P:N, :], x[0:LAST, NT - 1, :]).then_inc(out_stored, 16)
            sp.wait_ge(out_stored, 16 * (NCH + 1))

        @block.gpsimd
        def _(pool):
            made = 0

            def link(ins):
                nonlocal made
                made += 1
                ins.then_inc(pool_made, 1)
                pool.wait_ge(pool_made, made)

            pool.memset(ident[:], 0.0)
            pool.memset(ident_h[:], 0.0)
            pool.memset(real[:], 1.0)
            pool.memset(count[:], 1.0)
            pool.memset(minus_half[:], -0.5)
            link(pool.memset(ones[:], 1.0))
            pool.affine_select(out=ident[:], in_=ident[:], compare_op=ALU.not_equal, fill=1.0, base=0,
                               pattern=[[-1, P]], channel_multiplier=1)
            pool.affine_select(out=ident_h[:], in_=ident_h[:], compare_op=ALU.not_equal, fill=1.0, base=0,
                               pattern=[[-1, P]], channel_multiplier=1)
            pool.affine_select(out=real[:], in_=real[:], compare_op=ALU.is_gt, fill=0.0, base=N,
                               pattern=[[-P, NT]], channel_multiplier=-1)
            pool.affine_select(out=count[:], in_=count[:], compare_op=ALU.not_equal, fill=float(N), base=-N,
                               pattern=[[P, NT]], channel_multiplier=1)
            pool.iota(iota_e[:], pattern=[[1, 16]], base=0, channel_multiplier=0,
                      allow_small_or_imprecise_dtypes=True).then_inc(consts_made, 1)
            for mask in mask_nat:
                pool.memset(mask[:, N:NP], 0.0)
            pool.memset(mask_last[:], 0.0).then_inc(mask_cleared, 1)

            def scales(name):
                for c, (c0, w) in enumerate(CHUNKS):
                    pool.wait_ge(var_made, NCH * NORMS[name] + c + 1)
                    tiles = slice(c0 // P, (c0 + w) // P)
                    link(pool.tensor_scalar(var_eps[:, tiles], moments[:, tiles, 1], 1.0, LN_EPS, ALU.mult, ALU.add))
                    pool.tensor_scalar(neg_mean[:, tiles], moments[:, tiles, 0], -1.0, 0.0, ALU.mult, ALU.add)
                    link(pool.tensor_tensor(rstd[:, tiles], var_eps[:, tiles], minus_half[:, tiles], ALU.pow))
                    pool.tensor_tensor(shift[:, tiles], neg_mean[:, tiles], rstd[:, tiles], ALU.mult).then_inc(rstd_made, 1)

            def shift_x(name):
                pool.wait_ge(xn_dve, NCH * (NORMS[name] + 1))
                pool.wait_ge(xn_act, NCH * (NORMS[name] + 1))
                if name == "G2":
                    pool.tensor_tensor(x[:], x[:], beta[:].unsqueeze(1).to_broadcast([P, NT, D]), ALU.add).then_inc(x_shifted, 1)
                else:
                    pool.tensor_scalar(x[:], x[:], 1.0, -1.0, ALU.mult, ALU.add).then_inc(x_shifted, 1)

            def add_relu(n):
                pool.wait_ge(x_shifted, [1, 2, 4][n])
                for b, t0, k in GROUPS:
                    pool.wait_ge(relu_made, NG * n + b + 1)
                    xs = x[:, t0:t0 + k, :]
                    pool.tensor_tensor(xs, xs, xn[:, t0:t0 + k, :], ALU.add).then_inc(relu_added, 1)

            def mixture(f):
                E, kind = MOES[f]
                base = EXPERTS_BEFORE[f]

                def low_halves(e, b):
                    pool.wait_ge(in_w_high, base + e + 1)
                    pool.tensor_tensor(w_lo[b][:, 0:SPLIT[f]], w_exp[b][:, 0:SPLIT[f]],
                                       w_hi[b][:, 0:SPLIT[f]].bitcast(F32), ALU.subtract).then_inc(in_w_split, 1)

                with pool.Fori(0, E // 2) as k:
                    low_halves(2 * k, 0)
                    low_halves(2 * k + 1, 1)

            for stage in NORMS:
                scales(stage)
                if stage == "G0":
                    for dst, src in gat_loads[2:]:
                        pool.dma_start(dst, src).then_inc(gat_in, 16)
                    for dst, src in param_loads:
                        pool.dma_start(dst, src).then_inc(params_in, 16)
                if stage in ("G0", "G1a", "G2", "G3"):
                    shift_x(stage)
                if stage in ("G0", "G1a", "G3"):
                    add_relu(("G0", "G1a", "G3").index(stage))
                if stage in ("F0", "F1", "F3"):
                    mixture(("F0", "F1", "F3").index(stage))

        @block.tensor
        def _(pe):
            def keep_clock(n, bank):
                for _ in range(n):
                    pe.matmul(ps[:, bank, :], ident_h[:], maskT[:, 0, 0:BANK], start=True, stop=True)

            def turn_masks():
                for t in range(NT):
                    half = 2 * (t % 2)
                    pe.wait_ge(mask_made, t + 1)
                    if t >= 2:
                        pe.wait_ge(mask_copied, t - 1)
                    out = ps[:, half:half + 2, :].rearrange("p b n -> p (b n)").bitcast(BF16)
                    mask = mask_nat[t % AHEAD] if t < NT - 1 else mask_last
                    for j in range(NT):
                        m = pe.transpose(out[:, cols(j)], mask[:, cols(j)], ident_h[:])
                    m.then_inc(mask_turned, 1)

            def rows_from_tiles(tiles, wait_chunk, use):
                for c, (c0, w) in enumerate(CHUNKS):
                    wait_chunk(c)
                    for t in range(c0 // P, (c0 + w) // P):
                        m = pe.transpose(ps[:, ROW_BANKS + c, (t % TPB) * P:(t % TPB + 1) * P], tiles[:, t, :], ident[:])
                    m.then_inc(rows_made, 1)
                    if c == 1:
                        use(0)
                for c in range(1, NCH):
                    use(c)

            def normed_rows(name, use=lambda c: None):
                if name != "G0":
                    keep_clock(KEEP_A, MISC)
                    pe.wait_ge(var_made, NCH * NORMS[name] + 1)
                    keep_clock(KEEP_B, MISC)
                def wait_chunk(c):
                    pe.wait_ge(xn_dve, NCH * NORMS[name] + c + 1)
                    pe.wait_ge(xn_act, NCH * NORMS[name] + c + 1)
                rows_from_tiles(xn, wait_chunk, use)

            def wait_input(name):
                pe.wait_ge(inT_made, NCH * (INPUTS[name] + 1))

            def wait_input_chunk(name, c):
                pe.wait_ge(inT_made, NCH * INPUTS[name] + c + 1)

            def f1_row(g, c):
                c0, w = CHUNKS[c]
                wait_input_chunk(GATS[g][0], c)
                pe.matmul(row_bank(c), wa1_rep[g][:], inT[:, c0:c0 + w], start=True, stop=True).then_inc(f1_made, 1)

            def values(g):
                def use(c):
                    wait_input_chunk(GATS[g][0], c)
                    if c == NCH - 1:
                        pe.wait_ge(sum_made, g + 1)
                    for t in range(CHUNKS[c][0] // P, sum(CHUNKS[c]) // P):
                        b, i = divmod(t, SLOTS)
                        m = pe.matmul(ps[:, b, i * AW:(i + 1) * AW], inT[:, cols(t)], w_gat[:, g, :], start=True, stop=True)
                        if i == SLOTS - 1 or t == NT - 1:
                            m.then_inc(wh_made, 1)
                return use

            def attention(g):
                name, alpha = GATS[g]
                a = SCORED.index(g) if alpha is not None else None

                if alpha is not None:
                    f1_row(g, 0)
                    pe.wait_ge(f2_top_made, a + 1)
                    pe.transpose(ps[0:1, MISC, 1:1 + P], f2_top[:], ident[:]).then_inc(f2_top_turned, 1)
                    f1_row(g, 1)
                    pe.wait_ge(f2_top_all_made, a + 1)
                    pe.matmul(ps[:, MISC, 0:1], ones[0:1, :], f2_top_all[:], start=True, stop=True).then_inc(f2_max_spread, 1)
                    for c in range(2, NCH):
                        f1_row(g, c)
                    pe.wait_ge(wh_copied, NG * (g + 1))
                    if g:
                        keep_clock(HEAD_KEEP, NG - 1)
                if alpha is None:
                    pe.wait_ge(mask_copied, NT)

                def neighbours(j, b, first=False, last=False):
                    if alpha is None:
                        left = maskT[:, bass.ds(j, 1), :].rearrange("p o n -> p (o n)")
                        rights = [part[:, bass.ds(j, 1), :].rearrange("p o n -> p (o n)") for part in wh_part]
                    else:
                        left = prob[b]
                        rights = [wh[:, bass.ds(j, 1), 0:AW].rearrange("p o n -> p (o n)")]
                        if not first:
                            pe.wait_ge(prob_made, (NCH + NT - 1) * a + NCH + j)
                    for bank, t0, n in GROUPS:
                        if first:
                            pe.wait_ge(wh_copied, NG * g + bank + 1)
                        for t in range(t0, t0 + n):
                            if first and alpha is not None and t % TPB == 0:
                                pe.wait_ge(prob_made, (NCH + NT - 1) * a + t // TPB + 1)
                            for q, right in enumerate(rights):
                                m = pe.matmul(ps[:, bank, (t - t0) * AW:(t - t0 + 1) * AW], left[:, cols(t)], right,
                                              start=first and t == t0 and q == 0, stop=last and q == len(rights) - 1,
                                              skip_group_check=True)
                        if last:
                            m.then_inc(att_made, 1)
                    if not last and alpha is not None:
                        m.then_inc(prob_used, 1)

                peeled = 1
                if alpha is None:
                    pe.wait_ge(wh_split, 5)
                neighbours(0, 0, first=True)
                if alpha is None:
                    peeled = SLOTS
                    for j in range(1, SLOTS):
                        neighbours(j, j % 2)
                    pe.wait_ge(wh_split, 10)
                with pe.Fori(0, (NT - 2 - peeled) // 2) as k:
                    neighbours(2 * k + peeled, 1)
                    neighbours(2 * k + peeled + 1, 0)
                neighbours(NT - 2, 1)
                neighbours(NT - 1, 0, last=True)

            def mixture(f):
                E, kind = MOES[f]
                base = EXPERTS_BEFORE[f]
                name = f"F{[0, 1, 3][f]}"

                def logits_of(src, tiles):
                    for t in tiles:
                        m = pe.matmul(ps[:, MISC, t * E:(t + 1) * E], src[:, cols(t)], gate_w[f][:], start=True, stop=True)
                    if t == NT - 1:
                        m.then_inc(logits_made, 1)

                def route(c):
                    c0, w = CHUNKS[c]
                    wait_input_chunk(name, c)
                    if kind != "relu2":
                        return logits_of(inT, range(c0 // P, (c0 + w) // P))
                    m = pe.matmul(ps[0:64, ROW_BANKS + c, 0:w], router_w1[:], inT[:, c0:c0 + w], start=True, stop=True)
                    if c == NCH - 1:
                        m.then_inc(router_rows, 1)

                if kind == "relu2":
                    normed_rows(name, route)
                    pe.wait_ge(router_h_made, 1)
                    logits_of(router_h, range(NT))
                else:
                    normed_rows(name)

                def product(out, left, right):
                    pe.matmul(out, left[0], right[0], start=True, stop=False)
                    pe.matmul(out, left[0], right[1], start=False, stop=False)
                    return pe.matmul(out, left[1], right[0], start=False, stop=True)

                def w_cols(b, lo):
                    return w_hi[b][:, lo:lo + P], w_lo[b][:, lo:lo + P]

                ring = 2 if kind == "silu" else 4

                def units(e, b, which, first=False):
                    if 0 in which:
                        pe.wait_ge(in_w_split, base + e + 1)
                    for u in which:
                        half, c = divmod(u, NCH)
                        c0, w = NODE_CHUNKS[c]
                        if first and u < NCH:
                            pe.wait_ge(in_lo_made, NCH * f + c + 1)
                            if u == 1:
                                wait_input(name)
                        if not (first and u < ring):
                            pe.wait_ge(hid_made, UNITS * (base + e) + u - ring + 1)
                        s = (UNITS * b + u) % ring
                        x_halves = in_hi[:, c0:c0 + w], in_lo[:, c0:c0 + w]
                        if kind == "relu2" and half == 1:
                            pe.wait_ge(hid_made, UNITS * (base + e) + c + 1)
                            m = pe.matmul(ps[:, 3 + s, 0:w], w_exp[b][:, P:2 * P], hid[b][:, 0, c0:c0 + w],
                                          start=True, stop=True)
                        elif kind == "silu":
                            product(ps[:, 3 + 2 * s, 0:w], w_cols(b, half * P), x_halves).then_inc(gate_made, 1)
                            m = product(ps[:, 4 + 2 * s, 0:w], w_cols(b, 256 + half * P), x_halves)
                        else:
                            m = product(ps[:, 3 + s, 0:w], w_cols(b, half * P), x_halves)
                        m.then_inc(unit_made, 1)

                def output(e, b, k, first=False):
                    pe.wait_ge(hid_made, UNITS * (base + e + 1))
                    pe.wait_ge(experts_out_in[b], OUT_LOADED_BEFORE[f] + 16 * (k + 1))
                    if not first:
                        pe.wait_ge(y_used, base - f + e)
                    halves = (1,) if kind == "relu2" else (0, 1)
                    for c, (c0, w) in enumerate(CHUNKS):
                        for t in range(c0 // P, (c0 + w) // P):
                            for q, half in enumerate(halves):
                                m = pe.matmul(tile_out(t, nodes_of(t)), hid[b][:, half, t * P:t * P + nodes_of(t)],
                                              w_exp[b][:, OUT_AT[f] + q * P:OUT_AT[f] + (q + 1) * P],
                                              start=q == 0, stop=q == len(halves) - 1)
                        m.then_inc(y_made if c < NCH - 1 else expert_used, 1)

                def step(e, b, k, first=False):
                    if kind == "relu2":
                        units(e, b, range(0, NCH))
                        output(e - 1, 1 - b, k + b - 1, first)
                        units(e, b, range(NCH, UNITS))
                    else:
                        units(e, b, range(UNITS))
                        output(e - 1, 1 - b, k + b - 1, first)

                units(0, 0, range(UNITS), first=True)
                if kind != "relu2":
                    for c in range(NCH):
                        route(c)
                step(1, 1, 0, first=True)
                if f == 0:
                    pe.wait_ge(weights_made, 2)
                    pe.matmul(ps[:, MISC, 0:AW + 1], w0_T[:], w1_ext[:], start=True, stop=True).then_inc(w01_made, 1)
                with pe.Fori(1, E // 2 - (f < 2)) as k:
                    step(2 * k, 0, k)
                    step(2 * k + 1, 1, k)
                if f < 2:
                    step(E - 2, 0, E // 2 - 1)
                    units(E - 1, 1, range(UNITS))
                    pe.wait_ge(hid_made, UNITS * (base + E))
                    pe.wait_ge(disp_made, f + 1)
                    for t in range(NT):
                        m = pe.transpose(ps[0:E, 3 + t // TPB, (t % TPB) * P:(t % TPB + 1) * P], disp[:, t, 0:E], ident[:])
                    m.then_inc(disp_turned, 1)
                    output(E - 2, 0, E // 2 - 1)
                    pe.wait_ge(dispT_made, f + 1)
                    for t in range(NT):
                        m = pe.matmul(ps[:, 3 + t // TPB, (t % TPB) * P:(t % TPB + 1) * P], dispT[0:E, cols(t)],
                                      bias_out[f][:], start=True, stop=True)
                    m.then_inc(bias_made, 1)
                output(E - 1, 1, E // 2 - 1)

            pe.wait_ge(consts_made, 1)
            normed_rows("G0")
            turn_masks()
            pe.wait_ge(weights_made, 1)
            pe.wait_ge(mask_copied, NT)
            for c in range(NCH):
                values(0)(c)
            attention(0)
            pe.wait_ge(params_in, PARAMS)
            mixture(0)

            pe.wait_ge(weights_made, 3)
            normed_rows("G1a", values(1))
            attention(1)
            for i in range(2):
                def wait_chunk(c):
                    tiles = sum(CHUNKS[c]) // P
                    pe.wait_ge(elu_made, NG * i + -(-tiles // SLOTS))
                rows_from_tiles(hp, wait_chunk, values(2 + i))
                attention(2 + i)
            mixture(1)
            normed_rows("G2", values(4))
            attention(4)
            pe.wait_ge(hp_made, NG * 5)
            for t in range(NT):
                pe.matmul(tile_out(t), ones[0:1, :], lin_b[:], start=t % TPB == 0, stop=False, skip_group_check=True)

            def linear(c):
                c0, w = CHUNKS[c]
                wait_input_chunk("F2", c)
                for t in range(c0 // P, (c0 + w) // P):
                    m = pe.matmul(tile_out(t), inT[:, cols(t)], lin_wT[:], start=False, stop=True, skip_group_check=True)
                m.then_inc(lin_made, 1)

            normed_rows("F2", linear)
            normed_rows("G3", values(5))
            attention(5)
            mixture(2)

        @block.scalar
        def _(act):
            chain = 0

            def copy_rows(name, chunks=range(NCH)):
                for c in chunks:
                    c0, w = CHUNKS[c]
                    act.wait_ge(rows_made, NCH * INPUTS[name] + c + 1)
                    if name not in SUMMED:
                        act.activation(inT[:, c0:c0 + w], row_bank(c), ACT.Copy).then_inc(inT_made, 1)
                        continue
                    real_w = min(w, N - c0)
                    ins = act.activation(inT[:, c0:c0 + real_w], ps[:, ROW_BANKS + c, 0:real_w], ACT.Copy,
                                         accum_out=sum_parts[:, c:c + 1])
                    if real_w < w:
                        ins = act.activation(inT[:, N + 1:c0 + w], ps[:, ROW_BANKS + c, real_w + 1:w], ACT.Copy)
                    ins.then_inc(inT_made, 1)

            def normalise(name, src, dst, c):
                act.wait_ge(rstd_made, NCH * NORMS[name] + c + 1)
                for t in halves(c)[1]:
                    ins = act.activation(dst[:, t, :], src[:, t, :], ACT.Identity, bias=shift[:, t:t + 1], scale=rstd[:, t:t + 1])
                ins.then_inc(xn_act, 1)

            def normed_rows(name):
                normalise(name, x, xn, 0)
                for c in range(1, NCH):
                    normalise(name, x, xn, c)
                    copy_rows(name, [c - 1])
                copy_rows(name, [NCH - 1])

            def attention(g):
                _, alpha = GATS[g]
                a = SCORED.index(g) if alpha is not None else None
                PROBS = NCH + NT - 1

                for b, t0, n in GROUPS:
                    act.wait_ge(wh_made, NG * g + b + 1)
                    act.activation(wh[:, t0:t0 + n, 1:AW + 1], tiles_in(b, n, AW), ACT.Copy).then_inc(wh_copied, 1)
                if alpha is None:
                    return
                act.wait_ge(f2_shifted, a + 1)
                act.activation(f2_exp[:], f2_shift[:], ACT.Exp).then_inc(f2_exp_made, 1)
                for c, (c0, w) in enumerate(CHUNKS):
                    act.wait_ge(f1_read, NCH * a + c + 1)
                    act.activation(low[0][:, c0:c0 + w], f1_pos[:, c0:c0 + w], ACT.Exp, bias=f2_alpha[:, 0:1],
                                   scale=alpha - 1.0).then_inc(low_made, 1)

                def lower(j, b, first=False):
                    if not first:
                        act.wait_ge(prob_made, PROBS * a + NCH + j - 2)
                    act.activation(low[b][:], f1_pos[:], ACT.Exp, bias=f2_alpha[:, bass.ds(j, 1)],
                                   scale=alpha - 1.0).then_inc(low_made, 1)

                lower(1, 1, first=True)
                with act.Fori(1, (NT - 1) // 2) as k:
                    lower(2 * k, 0)
                    lower(2 * k + 1, 1)
                lower(NT - 1, 0)
                for b, t0, n in GROUPS:
                    act.wait_ge(hp_made, NG * (a + (g > 4)) + b + 1)
                    act.activation(hp_exp[:, t0:t0 + n, :], hp[:, t0:t0 + n, :], ACT.Exp).then_inc(hp_exp_made, 1)
                    if g in ADDED_ELU:
                        act.activation(xn[:, t0:t0 + n, :], hp[:, t0:t0 + n, :], ACT.Relu).then_inc(relu_made, 1)

            def mixture(f):
                E, kind = MOES[f]
                base = EXPERTS_BEFORE[f]
                exps = [0, 1, 3][f]
                def high_in(e, b, k, first=False):
                    act.wait_ge(experts_in[b], LOADED_BEFORE[f] + 16 * LOADS[f] * (k + 1))
                    if not first or f > 0:
                        act.wait_ge(unit_made, UNITS * (base + e - 1))
                    act.activation(w_hi[b][:, 0:SPLIT[f]], w_exp[b][:, 0:SPLIT[f]], ACT.Copy).then_inc(in_w_high, 1)

                def router_exp(k):
                    act.wait_ge(top_diff_made, [0, 1, 3][f] + k + 1)
                    if kind == "relu2" and k == 0:
                        act.activation(route_exp[:, :, 0:E], logits[:, :, 0:E], ACT.Exp)
                    act.activation(top_w[:, :, 1], top_w[:, :, 0], ACT.Exp).then_inc(top_exp_made, 1)

                def units(e, b, k, first=False, last=False):
                    if kind != "silu" and (not first or f > 0):
                        act.wait_ge(expert_used, base + e - 1)
                    for u in range(UNITS):
                        half, c = divmod(u, NCH)
                        c0, w = NODE_CHUNKS[c]
                        if kind == "silu":
                            s = u % 2
                            act.wait_ge(gate_made, UNITS * e + u + 1)
                            if not first or b or u >= 2:
                                act.wait_ge(hid_made, UNITS * (base + e) + u - 1)
                            act.activation(silu[s][:, 0:w], ps[:, 3 + 2 * s, 0:w], ACT.Silu).then_inc(silu_made, 1)
                        else:
                            act.wait_ge(unit_made, UNITS * (base + e) + u + 1)
                            s = (UNITS * b + u) % 4
                            bias = w_exp[b][:, BIAS_AT + half:BIAS_AT + half + 1]
                            act.activation(hid[b][:, half, c0:c0 + w], ps[:, 3 + s, 0:w], ACT.Relu,
                                           bias=bias).then_inc(hid_made, 1)
                        if first and not b and kind == "relu2" and u in (1, NCH):
                            router_exp(u // NCH)
                        if u == NCH - 1 and not last:
                            high_in(e + 1, 1 - b, k + b, first and b == 0)

                high_in(0, 0, 0, first=True)
                normed_rows(("F0", "F1", "F3")[f])
                if kind == "relu2":
                    act.wait_ge(router_rows, 1)
                    rows = ps[0:64, ROW_BANKS:ROW_BANKS + NCH, :].rearrange("p b n -> p (b n)")[:, 0:NP]
                    act.activation(router_h[:], rows, ACT.Relu, bias=router_b1[:]).then_inc(router_h_made, 1)
                units(0, 0, 0, first=True)
                units(1, 1, 0, first=True)
                if kind != "relu2":
                    router_exp(0)
                if kind == "silu":
                    act.activation(table_scratch[:], ones[:, 0:1], ACT.Silu)
                with act.Fori(1, E // 2 - 1) as k:
                    units(2 * k, 0, k)
                    units(2 * k + 1, 1, k)
                units(E - 2, 0, E // 2 - 1)
                units(E - 1, 1, E // 2 - 1, last=True)
                if f < 2:
                    act.wait_ge(disp_turned, f + 1)
                    rows = ps[0:E, 3:3 + NCH, :].rearrange("p b n -> p (b n)")[:, 0:NP]
                    act.activation(dispT[0:E, :], rows, ACT.Copy).then_inc(dispT_made, 1)

            for dst, src in gat_loads[:2]:
                act.dma_start(dst, src).then_inc(gat0_in, 16)
            normed_rows("G0")
            for t in range(NT):
                act.wait_ge(adj_used, t + 1)
                if t:
                    act.wait_ge(degree_made, t)
                mask = mask_nat[t % AHEAD] if t < NT - 1 else mask_last
                act.activation(count_junk, mask[:, 0:N], ACT.Copy, accum_out=degree[:, t:t + 1]).then_inc(degree_made, 1)
            attention(0)
            mixture(0)
            normed_rows("G1a")
            attention(1)
            copy_rows("G1b")
            attention(2)
            copy_rows("G1c")
            attention(3)
            mixture(1)
            normed_rows("G2")
            attention(4)
            for c in range(NCH):
                normalise("in G2", hp, hp_exp, c)
            normed_rows("F2")
            normed_rows("G3")
            attention(5)
            mixture(2)

        @block.vector
        def _(dve):
            chain = 0

            def link(ins):
                nonlocal chain
                chain += 1
                ins.then_inc(dve_done, 1)
                dve.wait_ge(dve_done, chain)

            def each(ap, n):
                return ap.unsqueeze(2).to_broadcast([P, ap.shape[1], n])

            def along_tiles(ap):
                return ap.unsqueeze(1).to_broadcast([P, NT, ap.shape[1]])

            def statistics(src, c):
                c0, w = CHUNKS[c]
                tiles = range(c0 // P, (c0 + w) // P)
                for t in tiles:
                    ins = dve.bn_stats(stats[:, t, :], src[:, t, :])
                link(ins)
                for t in tiles:
                    ins = dve.bn_aggr(moments[:, t, :], stats[:, t, :])
                ins.then_inc(var_made, 1)

            def apply(name, src, dst, c):
                dve.wait_ge(rstd_made, NCH * NORMS[name] + c + 1)
                for t in halves(c)[0]:
                    ins = dve.tensor_scalar(dst[:, t, :], src[:, t, :], moments[:, t, 0:1], rstd[:, t:t + 1],
                                            ALU.subtract, ALU.mult)
                ins.then_inc(xn_dve, 1)

            def normalise(name, before=lambda c: None, src=x, dst=xn):
                before(0)
                statistics(src, 0)
                for c in range(1, NCH):
                    before(c)
                    statistics(src, c)
                    apply(name, src, dst, c - 1)
                apply(name, src, dst, NCH - 1)

            def attention(g, then=None):
                name, alpha = GATS[g]
                a = SCORED.index(g) if alpha is not None else None
                PROBS = NCH + NT - 1
                dve.wait_ge(inT_made, NCH * (INPUTS[name] + 1))
                dve.reduce_sum(inT[:, N:N + 1], sum_parts[:], AX_X).then_inc(sum_made, 1)
                if alpha is None:
                    for i, tiles in enumerate((slice(0, SLOTS), slice(SLOTS, NT))):
                        dve.wait_ge(wh_copied, NG * g + (1 if i == 0 else NG))
                        rest = wh[:, tiles, 0:AW]
                        for q in range(3):
                            dve.tensor_copy(wh_part[q][:, tiles, :], rest).then_inc(wh_split, 1)
                            if q < 2:
                                dve.wait_ge(wh_split, 5 * i + 2 * q + 1)
                                dve.tensor_tensor(wh_rest[:, tiles, :], rest, wh_part[q][:, tiles, :],
                                                  ALU.subtract).then_inc(wh_split, 1)
                                dve.wait_ge(wh_split, 5 * i + 2 * q + 2)
                                rest = wh_rest[:, tiles, :]
                else:
                    dve.wait_ge(wh_copied, NG * (g + 1))
                    f2 = wh[:, :, AW]
                    link(dve.tensor_reduce(f2_top[:], f2[:, 0:NT - 1], AX_X, ALU.max))
                    dve.tensor_tensor(f2_top[0:LAST, :], f2_top[0:LAST, :], f2[0:LAST, NT - 1:NT], ALU.max).then_inc(f2_top_made, 1)
                    dve.wait_ge(f2_top_turned, a + 1)
                    dve.tensor_reduce(f2_top_all[:], ps[0:1, MISC, 1:1 + P], AX_X, ALU.max).then_inc(f2_top_all_made, 1)
                    dve.wait_ge(f2_max_spread, a + 1)
                    link(dve.scalar_tensor_tensor(f2_shift[:], f2, f2_max, real[:], ALU.subtract, ALU.mult))

                    def positive(c):
                        c0, w = CHUNKS[c]
                        dve.wait_ge(f1_made, NCH * a + c + 1)
                        dve.tensor_scalar(f1_pos[:, c0:c0 + w], row_bank(c), f2_max, 0.0, ALU.add, ALU.max).then_inc(f1_read, 1)

                    positive(0)
                    dve.tensor_scalar(f2_alpha[:], f2_shift[:], alpha, None, ALU.mult).then_inc(f2_shifted, 1)
                    positive(1)
                    dve.wait_ge(f2_exp_made, a + 1)
                    for c, (c0, w) in enumerate(CHUNKS):
                        dve.wait_ge(low_made, PROBS * a + c + 1)
                        dve.scalar_tensor_tensor(prob[0][:, c0:c0 + w], low[0][:, c0:c0 + w], f2_exp[:, 0:1],
                                                 maskT[:, 0, c0:c0 + w], ALU.max, ALU.mult).then_inc(prob_made, 1)
                        if c + 2 < NCH:
                            positive(c + 2)

                    def weights(j, b, first=False):
                        if not first:
                            dve.wait_ge(prob_used, (NT - 1) * a + j - 1)
                        mask = maskT[:, bass.ds(j, 1), :].rearrange("p o n -> p (o n)")
                        dve.wait_ge(low_made, PROBS * a + NCH + j)
                        dve.scalar_tensor_tensor(prob[b][:], low[b][:], f2_exp[:, bass.ds(j, 1)], mask,
                                                 ALU.max, ALU.mult).then_inc(prob_made, 1)

                    weights(1, 1, first=True)
                    with dve.Fori(1, (NT - 1) // 2) as k:
                        weights(2 * k, 0)
                        weights(2 * k + 1, 1)
                    weights(NT - 1, 0)
                def divide(b):
                    _, t0, n = GROUPS[b]
                    dve.wait_ge(att_made, NG * g + b + 1)
                    acc = tiles_in(b, n, AW)
                    link(dve.reciprocal(inv_sum[:, t0:t0 + n], acc[:, :, 0]))
                    dve.tensor_tensor(hp[:, t0:t0 + n, :], acc[:, :, 1:AW], each(inv_sum[:, t0:t0 + n], D),
                                      ALU.mult).then_inc(hp_made, 1)

                if then is None and alpha is not None:
                    divide(0)
                    for b, t0, n in GROUPS:
                        if b + 1 < NG:
                            divide(b + 1)
                        dve.wait_ge(hp_exp_made, NG * a + b + 1)
                        e = hp_exp[:, t0:t0 + n, :]
                        h = hp[:, t0:t0 + n, :]
                        link(dve.tensor_scalar(e, e, 1.0, -1.0, ALU.min, ALU.add))
                        dve.tensor_tensor(h, h, e, ALU.max).then_inc(elu_made, 1)
                    return
                for b in range(NG):
                    divide(b)
                if alpha is None:
                    dve.wait_ge(hp_made, NG * (g + 1))
                    return
                added = 0

                def add_elu(c):
                    nonlocal added
                    while added * SLOTS < sum(CHUNKS[c]) // P:
                        b, t0, n = GROUPS[added]
                        xs = x[:, t0:t0 + n, :]
                        dve.wait_ge(hp_exp_made, NG * a + b + 1)
                        dve.wait_ge(relu_added, NG * ADDED_ELU.index(g) + b + 1)
                        link(dve.scalar_tensor_tensor(xs, hp_exp[:, t0:t0 + n, :], 1.0, xs, ALU.min, ALU.add))
                        added += 1

                normalise(then, add_elu)

            def mixture(f, then=None):
                E, kind = MOES[f]
                base = EXPERTS_BEFORE[f]
                exps = [0, 1, 3][f]
                lg = logits[:, :, 0:E]
                wide = max(E, 8)
                for c, (c0, w) in enumerate(CHUNKS):
                    dve.wait_ge(inT_made, NCH * INPUTS[("F0", "F1", "F3")[f]] + c + 1)
                    dve.tensor_copy(in_hi[:, c0:c0 + w], inT[:, c0:c0 + w]).then_inc(in_hi_made, 1)
                    dve.wait_ge(in_hi_made, NCH * f + c + 1)
                    dve.tensor_tensor(in_lo[:, c0:c0 + w], inT[:, c0:c0 + w], in_hi[:, c0:c0 + w].bitcast(F32),
                                      ALU.subtract).then_inc(in_lo_made, 1)
                def units(e, b):
                    for u in range(UNITS if kind == "silu" else 0):
                        half, c = divmod(u, NCH)
                        c0, w = NODE_CHUNKS[c]
                        dve.wait_ge(silu_made, UNITS * e + u + 1)
                        dve.wait_ge(unit_made, UNITS * (base + e) + u + 1)
                        dve.tensor_tensor(hid[b][:, half, c0:c0 + w], silu[u % 2][:, 0:w],
                                          ps[:, 4 + 2 * (u % 2), 0:w], ALU.mult).then_inc(hid_made, 1)

                def combine(e, first=False, chunks=range(NCH), last=False):
                    if not first:
                        dve.wait_ge(y_used, base - f + e)
                    for c in chunks:
                        c0, w = CHUNKS[c]
                        if c < NCH - 1:
                            dve.wait_ge(y_made, (NCH - 1) * (base + e) + c + 1)
                        else:
                            dve.wait_ge(expert_used, base + e + 1)
                        for t in range(c0 // P, (c0 + w) // P):
                            r = nodes_of(t)
                            ins = dve.scalar_tensor_tensor(x[0:r, t, :], tile_out(t, r), disp[0:r, t, bass.ds(e, 1)],
                                                           x[0:r, t, :], ALU.mult, ALU.add)
                        if last and f == 2:
                            ins.then_inc(x_done, 1)
                        elif last:
                            link(ins)
                    if not last:
                        ins.then_inc(y_used, 1)

                units(0, 0)
                dve.wait_ge(logits_made, f + 1)
                if wide > E:
                    dve.memset(logits[:, :, E:wide], -1e30)
                link(dve.tensor_tensor(lg, tiles_in(MISC, NT, E), along_tiles(gate_b[f][:]), ALU.add))
                if f == 0:
                    link(dve.tensor_tensor(lg, lg, along_tiles(gate_b_more[:]), ALU.add))
                for t in range(NT):
                    ins = dve.max(top[:, t, :], logits[:, t, 0:wide])
                link(ins)
                for t in range(NT):
                    ins = dve.max_index(top_at[:, t, :], top[:, t, :], logits[:, t, 0:wide])
                link(ins)
                link(dve.tensor_copy(top_at_f[:, :, 0:2], top_at[:, :, 0:2]))
                if kind == "relu2":
                    link(dve.tensor_tensor(lg, lg, each(top[:, :, 0], E), ALU.subtract))
                    dve.tensor_tensor(top_w[:, :, 0], top[:, :, 1], top[:, :, 0], ALU.subtract).then_inc(top_diff_made, 1)
                    exps += 1
                    dve.wait_ge(top_exp_made, exps)
                    link(dve.reduce_sum(route_sum[:], route_exp[:, :, 0:E], AX_X))
                    link(dve.reciprocal(top_w[:, :, 2], route_sum[:]))
                    link(dve.tensor_scalar(top_w[:, :, 1], top_w[:, :, 1], -1.0, None, ALU.add))
                    dve.tensor_tensor(top_w[:, :, 0], top_w[:, :, 1], top_w[:, :, 2], ALU.mult).then_inc(top_diff_made, 1)
                else:
                    dve.tensor_tensor(top_w[:, :, 0], top[:, :, 1], top[:, :, 0], ALU.subtract).then_inc(top_diff_made, 1)
                units(1, 1)
                dve.wait_ge(top_exp_made, exps + 1)
                link(dve.tensor_scalar(top_w[:, :, 3], top_w[:, :, 1], 1.0, None, ALU.add))
                link(dve.reciprocal(top_w[:, :, 2], top_w[:, :, 3]))
                link(dve.tensor_tensor(top_w[:, :, 3], top_w[:, :, 1], top_w[:, :, 2], ALU.mult))
                places = along_tiles(iota_e[:, 0:E])
                for q, dst in enumerate((disp, disp_2)):
                    link(dve.tensor_tensor(dst[:, :, 0:E], places, each(top_at_f[:, :, q], E), ALU.is_equal))
                    link(dve.tensor_tensor(dst[:, :, 0:E], dst[:, :, 0:E], each(top_w[:, :, 2 + q], E), ALU.mult))
                dve.tensor_tensor(disp[:, :, 0:E], disp[:, :, 0:E], disp_2[:, :, 0:E], ALU.add).then_inc(disp_made, 1)
                dve.wait_ge(disp_made, f + 1)

                if f == 0:
                    dve.wait_ge(gat_in, GAT_LOADED)
                    dve.tensor_copy(w1_ext[:, 0:D], w_gat[:, 1, 0:D])
                    for h, dst in enumerate((w1_ext[:, AW:AW + 1], w1_ext[:, D:AW])):
                        project(1, h, dst)
                    for g in SCORED[2:]:
                        ins = attention_weights(g)
                    ins.then_inc(weights_made, 1)

                def step(e, b, first=False):
                    if not first:
                        units(e, b)
                    combine(e - 1, first)

                step(1, 1, first=True)
                if f == 0:
                    dve.wait_ge(w01_made, 1)
                    dve.tensor_copy(w_gat[:, 1, :], ps[:, MISC, 0:AW])
                    link(dve.tensor_copy(wa1[:, 1:2], ps[:, MISC, AW:AW + 1]))
                    dve.tensor_scalar(wa1_rep[1][:], ones[:], wa1[:, 1:2], None, ALU.mult).then_inc(weights_made, 1)
                with dve.Fori(1, E // 2) as k:
                    step(2 * k, 0)
                    step(2 * k + 1, 1)
                if f < 2:
                    dve.wait_ge(bias_made, f + 1)
                    dve.wait_ge(y_used, base - f + E - 1)
                    dve.tensor_tensor(x[:], x[:], ps[:, 3:3 + NCH, :].rearrange("p b n -> p (b n)")[:, 0:NP]
                                      .rearrange("p (t d) -> p t d", d=D), ALU.add).then_inc(bias_added, 1)
                    dve.wait_ge(bias_added, f + 1)
                if then is None:
                    combine(E - 1, last=True)
                else:
                    normalise(then, lambda c: combine(E - 1, chunks=[c], last=True))

            def project(g, h, dst):
                link(dve.tensor_tensor_reduce(dot_junk[:], w_gat[:, g, 0:D], a_row[g][:, h * D:(h + 1) * D], 1.0, 0.0,
                                              ALU.mult, ALU.add, dst))

            def attention_weights(g):
                project(g, 0, wa1[:, g:g + 1])
                project(g, 1, w_gat[:, g, D:D + 1])
                return dve.tensor_scalar(wa1_rep[g][:], ones[:], wa1[:, g:g + 1], None, ALU.mult)

            dve.memset(x[:, NT - 1, :], 0.0).then_inc(pad_cleared, 1)
            dve.wait_ge(x_in, X_LOADS)
            normalise("G0")
            dve.wait_ge(gat0_in, 32)
            dve.wait_ge(consts_made, 1)
            dve.tensor_copy(wh[:, :, 0], count[:])
            dve.memset(w_gat[:, 4, D:AW], 0.0)
            attention_weights(0).then_inc(weights_made, 1)

            def make(t):
                dve.wait_ge(adj_in[t % ADJ_AHEAD], 16 * (t // ADJ_AHEAD + 1))
                rows = P if t < NT - 1 else LAST
                mask = mask_nat[t % AHEAD] if t < NT - 1 else mask_last
                if t >= AHEAD:
                    dve.wait_ge(mask_turned, t - AHEAD + 1)
                dve.tensor_scalar(mask[0:rows, 0:N], adj_i[t % ADJ_AHEAD][0:rows, :], 0, None, ALU.is_gt).then_inc(adj_used, 1)

            def finish(t):
                dve.wait_ge(degree_made, t + 1)
                mask = mask_nat[t % AHEAD] if t < NT - 1 else mask_last
                dve.tensor_scalar(mask[:, N:N + 1], degree[:, t:t + 1], 0.0, None, ALU.is_equal).then_inc(mask_made, 1)

            def copy_out(t):
                dve.wait_ge(mask_turned, t + 1)
                half = 2 * (t % 2)
                src = ps[:, half:half + 2, :].rearrange("p b n -> p (b n)").bitcast(BF16)[:, 0:NP]
                dve.tensor_copy(maskT[:, :, cols(t)], src.rearrange("p (j n) -> p j n", n=P)).then_inc(mask_copied, 1)

            dve.wait_ge(mask_cleared, 1)
            for t in range(AHEAD - 1):
                make(t)
            for t in range(NT):
                finish(t)
                if t:
                    copy_out(t - 1)
                if t + AHEAD - 1 < NT:
                    make(t + AHEAD - 1)
            copy_out(NT - 1)

            attention(0, "F0")
            mixture(0, "G1a")
            attention(1)
            attention(2)
            attention(3, "F1")
            mixture(1, "G2")
            attention(4)

            def finish_l2(c):
                c0, w = CHUNKS[c]
                part = slice(c0 // P, (c0 + w) // P)
                dve.wait_ge(xn_act, NCH * NORMS["in G2"] + c + 1)
                dve.wait_ge(xn_dve, NCH * NORMS["in G2"] + c + 1)
                n = part.stop - part.start
                e = hp_exp[:, part, :]
                link(dve.tensor_tensor(e, e, gamma[:].unsqueeze(1).to_broadcast([P, n, D]), ALU.mult))
                link(dve.tensor_tensor(x[:, part, :], x[:, part, :], e, ALU.add))

            normalise("in G2", src=hp, dst=hp_exp)
            dve.wait_ge(x_shifted, 3)
            normalise("F2", finish_l2)

            def add_linear(c):
                c0, w = CHUNKS[c]
                dve.wait_ge(lin_made, c + 1)
                part = slice(c0 // P, (c0 + w) // P)
                out = ps[:, c, 0:w].rearrange("p (t d) -> p t d", d=D)
                link(dve.tensor_tensor(x[:, part, :], x[:, part, :], out, ALU.add))

            normalise("G3", add_linear)
            attention(5, "F3")
            mixture(2)


OUTPUT = "out"


def kernel(**inputs):
    import numpy as np
    import concourse.bacc as bacc
    from concourse.bass_utils import run_bass_kernel_spmd

    nc = bacc.Bacc("TRN2", target_bir_lowering=False, num_devices=1)
    arrays, io = {}, {}
    for name, value in inputs.items():
        if name == "L1_ffn_expert_b2":
            continue
        if name == "L2_gnn_a":
            continue
        a = np.asarray(value)
        if name == "L0_ffn_b1":
            a = a.reshape(a.shape[0], 2, P).transpose(0, 2, 1)
        elif name == "L1_ffn_expert_b1":
            name, a = "L1_ffn_expert_b12", np.stack([a, np.asarray(inputs["L1_ffn_expert_b2"])], axis=-1)
        elif name in ("L2_ffn_weight", "L1_gnn_W0"):
            a = a.T
        a = np.ascontiguousarray(a)
        arrays[f"in_{name}"] = a
        io[name] = nc.dram_tensor(f"in_{name}", a.shape, mybir.dt.from_np(a.dtype), kind="ExternalInput").ap()
    io["out"] = nc.dram_tensor("out", inputs["x"].shape, F32, kind="ExternalOutput").ap()
    build(nc, io)
    result = run_bass_kernel_spmd(nc, [arrays], core_ids=[0])
    return result.results[0]["out"]
```
